# Optimizing a Trainium2 kernel written in Bass

```python
import numpy as np
import jax
import jax.numpy as jnp

def _softmax(x, axis=-1):
    return jax.nn.softmax(x, axis=axis)

def _gelu(x):
    return jax.nn.gelu(x, approximate=True)

def _silu(x):
    return jax.nn.silu(x)

def _sigmoid(x):
    return jax.nn.sigmoid(x)

def _layernorm(x, axis=-1, eps=1e-05):
    m = jnp.mean(x, axis=axis, keepdims=True)
    v = jnp.var(x, axis=axis, keepdims=True)
    return (x - m) / jnp.sqrt(v + eps)

def _scatter_add(tgt, idx, src, axis=0):
    return tgt.at[idx].add(src)

def _segment_sum(src, seg, n):
    return jax.ops.segment_sum(src, seg, n)
kernel_name = 'mk_seq_preln_d2_jaxref_r8_e8bea5'

def setup_inputs(seed: int=0):
    np.random.seed(seed)
    _w = jnp.asarray

    def _L0_attn_setup():
        import jax, jax.numpy as jnp
        import numpy as np
        EMBED_DIM = 256
        NUM_HEADS = 16
        HEAD_DIM = EMBED_DIM // NUM_HEADS
        SEQ_LEN = 256
        BATCH = 2
        ROPE_BASE = 10000.0

        def rope_cache(seq_len, dim, dtype=jnp.float32):
            inv_freq = 1.0 / ROPE_BASE ** (np.arange(0, dim, 2, dtype=np.float32) / dim)
            pos = np.arange(seq_len, dtype=np.float32)
            freqs = np.outer(pos, inv_freq)
            emb = np.concatenate([freqs, freqs], axis=-1)
            return (jnp.asarray(np.cos(emb), dtype), jnp.asarray(np.sin(emb), dtype))

        def rotate_half(x):
            x1, x2 = jnp.split(x, 2, axis=-1)
            return jnp.concatenate([-x2, x1], axis=-1)
        key = jax.random.key(seed)
        ks = jax.random.split(key, 9)
        s = 1.0 / np.sqrt(EMBED_DIM)

        def lin(kw, kb):
            W = jax.random.uniform(kw, (EMBED_DIM, EMBED_DIM), jnp.float32, -s, s)
            b = jax.random.uniform(kb, (EMBED_DIM,), jnp.float32, -s, s)
            return (W, b)
        Wq, bq = lin(ks[0], ks[1])
        Wk, bk = lin(ks[2], ks[3])
        Wv, bv = lin(ks[4], ks[5])
        Wo, bo = lin(ks[6], ks[7])
        x = jax.random.normal(ks[8], (BATCH, SEQ_LEN, EMBED_DIM), jnp.float32)
        return {'x': x, 'Wq': Wq, 'bq': bq, 'Wk': Wk, 'bk': bk, 'Wv': Wv, 'bv': bv, 'Wo': Wo, 'bo': bo}
    _L0_attn_in = _L0_attn_setup()

    def _L0_ffn_setup():
        import jax, jax.numpy as jnp
        import numpy as np
        NUM_EXPERTS = 16
        TOP_K = 4
        N_GROUP = 4
        TOPK_GROUP = 2
        SCALING = 2.5

        def _route(x, gate_weight, expert_bias):
            logits = x @ gate_weight.T
            scores = jax.nn.sigmoid(logits)
            biased = scores + expert_bias[None, :]
            T = x.shape[0]
            gsz = NUM_EXPERTS // N_GROUP
            grp = biased.reshape(T, N_GROUP, gsz)
            top2, _ = jax.lax.top_k(grp, 2)
            group_scores = top2.sum(-1)
            _, gidx = jax.lax.top_k(group_scores, TOPK_GROUP)
            gmask = jax.nn.one_hot(gidx, N_GROUP, dtype=scores.dtype).sum(1)
            emask = jnp.repeat(gmask, gsz, axis=1)
            masked = jnp.where(emask > 0, biased, -jnp.inf)
            _, sel = jax.lax.top_k(masked, TOP_K)
            w = jnp.take_along_axis(scores, sel, axis=1)
            w = w / (w.sum(-1, keepdims=True) + 1e-20)
            return (w * SCALING, sel)

        def _moe(x, w, sel, gate_proj, up_proj, down_proj):
            cw = (jax.nn.one_hot(sel, NUM_EXPERTS, dtype=x.dtype) * w[..., None]).sum(1)

            def body(acc, inp):
                g, u, d, we = inp
                y = jax.nn.silu(x @ g.T) * (x @ u.T) @ d.T
                return (acc + we[:, None] * y, None)
            out, _ = jax.lax.scan(body, jnp.zeros_like(x), (gate_proj, up_proj, down_proj, cw.T))
            return out
        key = jax.random.key(seed)
        ks = jax.random.split(key, 9)
        B, S, H, I = (2, 128, 256, 128)
        w = lambda k, shape: jax.random.normal(k, shape, jnp.float32) * 0.02
        return {'hidden_states': jax.random.normal(ks[0], (B, S, H), jnp.float32), 'gate_weight': w(ks[1], (NUM_EXPERTS, H)), 'expert_bias': jnp.zeros((NUM_EXPERTS,), jnp.float32), 'gate_proj': w(ks[2], (NUM_EXPERTS, I, H)), 'up_proj': w(ks[3], (NUM_EXPERTS, I, H)), 'down_proj': w(ks[4], (NUM_EXPERTS, H, I)), 'shared_gate': w(ks[5], (I, H)), 'shared_up': w(ks[6], (I, H)), 'shared_down': w(ks[7], (H, I))}
    _L0_ffn_in = _L0_ffn_setup()

    def _L1_attn_setup():
        import jax, jax.numpy as jnp
        import numpy as np
        B, T, C = (4, 256, 256)
        NUM_HEADS = 16
        HEAD_SIZE = C // NUM_HEADS
        key = jax.random.key(seed)
        ks = jax.random.split(key, 5)
        scale = 0.02
        return {'x': jax.random.normal(ks[0], (B, T, C), dtype=jnp.float32), 'w_qkv': jax.random.normal(ks[1], (C, 3 * NUM_HEADS * HEAD_SIZE), dtype=jnp.float32) * scale, 'b_qkv': jax.random.normal(ks[2], (3 * NUM_HEADS * HEAD_SIZE,), dtype=jnp.float32) * scale, 'w_proj': jax.random.normal(ks[3], (NUM_HEADS * HEAD_SIZE, C), dtype=jnp.float32) * scale, 'b_proj': jax.random.normal(ks[4], (C,), dtype=jnp.float32) * scale}
    _L1_attn_in = _L1_attn_setup()

    def _L1_ffn_setup():
        import jax, jax.numpy as jnp
        import numpy as np
        HIDDEN = 256
        INTER = 704
        B, S = (2, 256)

        def _ternary(key, shape):
            return jax.random.randint(key, shape, -1, 2).astype(jnp.float32)
        key = jax.random.key(seed)
        ks = jax.random.split(key, 7)
        x = jax.random.normal(ks[0], (B, S, HIDDEN), dtype=jnp.float32)
        gate_w = _ternary(ks[1], (INTER, HIDDEN))
        up_w = _ternary(ks[2], (INTER, HIDDEN))
        down_w = _ternary(ks[3], (HIDDEN, INTER))
        gate_s = jax.random.uniform(ks[4], (INTER,), minval=0.01, maxval=0.1, dtype=jnp.float32)
        up_s = jax.random.uniform(ks[5], (INTER,), minval=0.01, maxval=0.1, dtype=jnp.float32)
        down_s = jax.random.uniform(ks[6], (HIDDEN,), minval=0.01, maxval=0.1, dtype=jnp.float32)
        return {'x': x, 'gate_w': gate_w, 'up_w': up_w, 'down_w': down_w, 'gate_s': gate_s, 'up_s': up_s, 'down_s': down_s}
    _L1_ffn_in = _L1_ffn_setup()
    _d = {'L0_attn_x': _L0_attn_in['x'], 'L0_attn_Wq': _L0_attn_in['Wq'], 'L0_attn_bq': _L0_attn_in['bq'], 'L0_attn_Wk': _L0_attn_in['Wk'], 'L0_attn_bk': _L0_attn_in['bk'], 'L0_attn_Wv': _L0_attn_in['Wv'], 'L0_attn_bv': _L0_attn_in['bv'], 'L0_attn_Wo': _L0_attn_in['Wo'], 'L0_attn_bo': _L0_attn_in['bo'], 'L0_ffn_gate_weight': _L0_ffn_in['gate_weight'], 'L0_ffn_expert_bias': _L0_ffn_in['expert_bias'], 'L0_ffn_gate_proj': _L0_ffn_in['gate_proj'], 'L0_ffn_up_proj': _L0_ffn_in['up_proj'], 'L0_ffn_down_proj': _L0_ffn_in['down_proj'], 'L0_ffn_shared_gate': _L0_ffn_in['shared_gate'], 'L0_ffn_shared_up': _L0_ffn_in['shared_up'], 'L0_ffn_shared_down': _L0_ffn_in['shared_down'], 'L1_attn_w_qkv': _L1_attn_in['w_qkv'], 'L1_attn_b_qkv': _L1_attn_in['b_qkv'], 'L1_attn_w_proj': _L1_attn_in['w_proj'], 'L1_attn_b_proj': _L1_attn_in['b_proj'], 'L1_ffn_gate_w': _L1_ffn_in['gate_w'], 'L1_ffn_up_w': _L1_ffn_in['up_w'], 'L1_ffn_down_w': _L1_ffn_in['down_w'], 'L1_ffn_gate_s': _L1_ffn_in['gate_s'], 'L1_ffn_up_s': _L1_ffn_in['up_s'], 'L1_ffn_down_s': _L1_ffn_in['down_s']}
    _x0 = _d['L0_attn_x']
    _d['L0_attn_x'] = jax.random.normal(jax.random.fold_in(jax.random.key(seed), 1), (2, 512, 256), dtype=_x0.dtype)
    del _x0
    return _d

def reference(L0_attn_x, L0_attn_Wq, L0_attn_bq, L0_attn_Wk, L0_attn_bk, L0_attn_Wv, L0_attn_bv, L0_attn_Wo, L0_attn_bo, L0_ffn_gate_weight, L0_ffn_expert_bias, L0_ffn_gate_proj, L0_ffn_up_proj, L0_ffn_down_proj, L0_ffn_shared_gate, L0_ffn_shared_up, L0_ffn_shared_down, L1_attn_w_qkv, L1_attn_b_qkv, L1_attn_w_proj, L1_attn_b_proj, L1_ffn_gate_w, L1_ffn_up_w, L1_ffn_down_w, L1_ffn_gate_s, L1_ffn_up_s, L1_ffn_down_s):

    def _L0_attn_ref(x, Wq, bq, Wk, bk, Wv, bv, Wo, bo):
        import jax, jax.numpy as jnp
        import numpy as np
        EMBED_DIM = 256
        NUM_HEADS = 16
        HEAD_DIM = EMBED_DIM // NUM_HEADS
        SEQ_LEN = 256
        BATCH = 2
        ROPE_BASE = 10000.0

        def rope_cache(seq_len, dim, dtype=jnp.float32):
            inv_freq = 1.0 / ROPE_BASE ** (np.arange(0, dim, 2, dtype=np.float32) / dim)
            pos = np.arange(seq_len, dtype=np.float32)
            freqs = np.outer(pos, inv_freq)
            emb = np.concatenate([freqs, freqs], axis=-1)
            return (jnp.asarray(np.cos(emb), dtype), jnp.asarray(np.sin(emb), dtype))

        def rotate_half(x):
            x1, x2 = jnp.split(x, 2, axis=-1)
            return jnp.concatenate([-x2, x1], axis=-1)
        B, S, E = x.shape
        H, D = (NUM_HEADS, HEAD_DIM)
        cos, sin = rope_cache(S, D, x.dtype)

        def heads(t):
            return t.reshape(B, S, H, D).transpose(0, 2, 1, 3)
        q = heads(x @ Wq.T + bq)
        k = heads(x @ Wk.T + bk)
        v = heads(x @ Wv.T + bv)
        q = q * cos + rotate_half(q) * sin
        k = k * cos + rotate_half(k) * sin
        scale = D ** (-0.5)
        attn = jnp.einsum('bhqd,bhkd->bhqk', q, k) * scale
        attn = jax.nn.softmax(attn, axis=-1)
        out = jnp.einsum('bhqk,bhkd->bhqd', attn, v)
        out = out.transpose(0, 2, 1, 3).reshape(B, S, E)
        return out @ Wo.T + bo

    def _L0_ffn_ref(hidden_states, gate_weight, expert_bias, gate_proj, up_proj, down_proj, shared_gate, shared_up, shared_down):
        import jax, jax.numpy as jnp
        import numpy as np
        NUM_EXPERTS = 16
        TOP_K = 4
        N_GROUP = 4
        TOPK_GROUP = 2
        SCALING = 2.5

        def _route(x, gate_weight, expert_bias):
            logits = x @ gate_weight.T
            scores = jax.nn.sigmoid(logits)
            biased = scores + expert_bias[None, :]
            T = x.shape[0]
            gsz = NUM_EXPERTS // N_GROUP
            grp = biased.reshape(T, N_GROUP, gsz)
            top2, _ = jax.lax.top_k(grp, 2)
            group_scores = top2.sum(-1)
            _, gidx = jax.lax.top_k(group_scores, TOPK_GROUP)
            gmask = jax.nn.one_hot(gidx, N_GROUP, dtype=scores.dtype).sum(1)
            emask = jnp.repeat(gmask, gsz, axis=1)
            masked = jnp.where(emask > 0, biased, -jnp.inf)
            _, sel = jax.lax.top_k(masked, TOP_K)
            w = jnp.take_along_axis(scores, sel, axis=1)
            w = w / (w.sum(-1, keepdims=True) + 1e-20)
            return (w * SCALING, sel)

        def _moe(x, w, sel, gate_proj, up_proj, down_proj):
            cw = (jax.nn.one_hot(sel, NUM_EXPERTS, dtype=x.dtype) * w[..., None]).sum(1)

            def body(acc, inp):
                g, u, d, we = inp
                y = jax.nn.silu(x @ g.T) * (x @ u.T) @ d.T
                return (acc + we[:, None] * y, None)
            out, _ = jax.lax.scan(body, jnp.zeros_like(x), (gate_proj, up_proj, down_proj, cw.T))
            return out
        B, S, H = hidden_states.shape
        x = hidden_states.reshape(-1, H)
        w, sel = _route(x, gate_weight, expert_bias)
        out = _moe(x, w, sel, gate_proj, up_proj, down_proj)
        shared = jax.nn.silu(x @ shared_gate.T) * (x @ shared_up.T) @ shared_down.T
        return (out + shared).reshape(B, S, H)

    def _L1_attn_ref(x, w_qkv, b_qkv, w_proj, b_proj):
        import jax, jax.numpy as jnp
        import numpy as np
        B, T, C = (4, 256, 256)
        NUM_HEADS = 16
        HEAD_SIZE = C // NUM_HEADS
        b, t, c = x.shape
        h, d = (NUM_HEADS, HEAD_SIZE)
        qkv = x @ w_qkv + b_qkv
        q, k, v = jnp.split(qkv, 3, axis=-1)
        q = q.reshape(b, t, h, d).transpose(0, 2, 1, 3)
        k = k.reshape(b, t, h, d).transpose(0, 2, 1, 3)
        v = v.reshape(b, t, h, d).transpose(0, 2, 1, 3)
        scores = jnp.einsum('bhqd,bhkd->bhqk', q, k) * d ** (-0.5)
        causal = jnp.tril(jnp.ones((t, t), dtype=bool))
        scores = jnp.where(causal, scores, jnp.float32(-jnp.inf))
        attn = jax.nn.softmax(scores, axis=-1)
        out = jnp.einsum('bhqk,bhkd->bhqd', attn, v)
        out = out.transpose(0, 2, 1, 3).reshape(b, t, h * d)
        return out @ w_proj + b_proj

    def _L1_ffn_ref(x, gate_w, up_w, down_w, gate_s, up_s, down_s):
        import jax, jax.numpy as jnp
        import numpy as np
        HIDDEN = 256
        INTER = 704
        B, S = (2, 256)

        def _ternary(key, shape):
            return jax.random.randint(key, shape, -1, 2).astype(jnp.float32)
        b, s, h = x.shape
        xf = x.reshape(b * s, h)
        g = jnp.einsum('th,ih->ti', xf, gate_w) * gate_s
        u = jnp.einsum('th,ih->ti', xf, up_w) * up_s
        hdn = jax.nn.silu(g) * u
        out = jnp.einsum('ti,hi->th', hdn, down_w) * down_s
        return out.reshape(b, s, -1)
    x = L0_attn_x
    x = x + _L0_attn_ref(_layernorm(x, axis=-1), L0_attn_Wq, L0_attn_bq, L0_attn_Wk, L0_attn_bk, L0_attn_Wv, L0_attn_bv, L0_attn_Wo, L0_attn_bo)
    x = x + _L0_ffn_ref(_layernorm(x, axis=-1), L0_ffn_gate_weight, L0_ffn_expert_bias, L0_ffn_gate_proj, L0_ffn_up_proj, L0_ffn_down_proj, L0_ffn_shared_gate, L0_ffn_shared_up, L0_ffn_shared_down)
    x = x + _L1_attn_ref(_layernorm(x, axis=-1), L1_attn_w_qkv, L1_attn_b_qkv, L1_attn_w_proj, L1_attn_b_proj)
    x = x + _L1_ffn_ref(_layernorm(x, axis=-1), L1_ffn_gate_w, L1_ffn_up_w, L1_ffn_down_w, L1_ffn_gate_s, L1_ffn_up_s, L1_ffn_down_s)
    return x

_drawn_inputs = setup_inputs


def setup_inputs(seed=0):
    import zlib

    import numpy as np

    out = dict(_drawn_inputs(seed))
    spreads = {'L0_ffn_expert_bias': (0.0, 0.481)}
    factors = {'L0_attn_Wq': 7.752,
     'L0_attn_bq': 8.0,
     'L0_attn_Wk': 7.778,
     'L0_attn_bk': 8.0,
     'L0_attn_Wv': 3.202,
     'L0_ffn_gate_weight': 5.12,
     'L0_ffn_gate_proj': 3.43,
     'L0_ffn_up_proj': 3.389,
     'L0_ffn_down_proj': 3.393,
     'L0_ffn_shared_gate': 4.387,
     'L0_ffn_shared_up': 4.318,
     'L0_ffn_shared_down': 4.311,
     'L1_attn_w_qkv': 4.079,
     'L1_attn_b_qkv': 6.859,
     'L1_attn_w_proj': 3.64,
     'L1_attn_b_proj': 5.695}
    for name, (base, spread) in spreads.items():
        noise = np.random.default_rng([zlib.crc32(name.encode()), seed]).standard_normal(out[name].shape)
        drawn = base * np.exp(spread * noise) if base else spread * noise
        out[name] = jnp.asarray(drawn.astype(out[name].dtype))
    for name, factor in factors.items():
        out[name] = (out[name] * factor).astype(out[name].dtype)
    return out
```

```python
from contextlib import ExitStack

import numpy as np

import concourse.bass as bass
from concourse import mybir

P = 128
BATCH, SEQ, DM = 2, 512, 256
TILES = BATCH * SEQ // P
TPB = SEQ // P
CH = DM // P
HEADS, HD = 16, 16
HPG = 4
GROUPS = BATCH * HEADS // HPG
GW = 3 * HPG * HD
SLOT = 64
EXPERTS, TOPK, INTER = 16, 4, 128
NGRP, GSZ = 4, 4
FFN_INTER = 704
FFN_CHUNKS = -(-FFN_INTER // P)
STREAM = 1 + EXPERTS + FFN_CHUNKS
WCOLS = 2 * CH * P + DM
SCALE = HD ** -0.5
EPS = 1e-5
NEG = -1e30

F32 = mybir.dt.float32
F32R = mybir.dt.float32r
ACT = mybir.ActivationFunctionType
ALU = mybir.AluOpType
AX = mybir.AxisListType
ds = bass.ds

BANK_S1, BANK_S2, BANK_O, BANK_T, BANK_P = (0, 1), (2, 3), 4, (5, 6), 7
BANK_G, BANK_U, BANK_Y = (0, 1), (2, 3), (4, 5, 6, 7)


def two_layers(nc, x, wqkv, bqkv, wo, bo, rope, masks, ident_in, router_w, router_b, ties, stream_w,
               stream_scale, down_scale, out):
    with ExitStack() as ctx:
        def sb(name, shape, dt=F32):
            return ctx.enter_context(nc.sbuf_tensor(name, shape, dt))

        def sem(name):
            return ctx.enter_context(nc.semaphore(name))

        X = sb("resid", [P, TILES, DM])
        XN = sb("normed", [P, TILES, DM])
        XT = [sb(f"xT_{n}", [P, CH, BATCH * SEQ], F32R) for n in ("hi", "lo")]
        stage_qkv = sb("stage_qkv", [P, CH, 3 * DM])
        WQKV = [sb(f"wqkv_{n}", [P, CH, 3 * DM], F32R) for n in ("hi", "lo")]
        stage_wo = sb("stage_wo", [P, CH, DM])
        WO = [sb(f"wo_{n}", [P, CH, DM], F32R) for n in ("hi", "lo")]
        BQKV = sb("b_qkv", [P, 3 * DM])
        BO = sb("b_o", [P, DM])
        ROPE = sb("rope_tables", [P, 2, TPB * HPG, HD])
        ident = sb("ident", [P, P])
        ident_r = sb("ident_r", [P, P], F32R)
        mask_in = sb("mask_in", [P, 2, P])
        mask_r = sb("mask_r", [P, 2, P], F32R)
        QK = [sb(f"qk{s}", [P, 2, TPB * HPG, HD]) for s in range(2)]
        ROT = sb("rotated", [P, 2, TPB * HPG, HD])
        ROPED = [sb(f"roped{s}", [P, 2, TPB * HPG, HD]) for s in range(2)]
        QS = [sb(f"q_stack{s}", [P, TPB * HPG, SLOT], F32R) for s in range(2)]
        KS = [sb(f"k_stack{s}", [P, TPB * HPG, SLOT], F32R) for s in range(2)]
        QT = [sb(f"qT{s}", [P, 2, SEQ], F32R) for s in range(2)]
        KT = [sb(f"kT{s}", [P, HPG, SEQ], F32R) for s in range(2)]
        VS = [sb(f"v_stack{s}", [P, TPB, HPG, 32]) for s in range(2)]
        NRING = 8
        VR = [sb(f"v{s}", [P, TPB, HPG * HD]) for s in range(2)]
        PT = sb("probsT", [P, NRING, SEQ])
        OS = sb("outT", [P, SEQ])
        MX = [sb(f"maxes{s}", [P, HPG, TPB]) for s in range(2)]
        RD = sb("rdenom", [P, TPB * HPG])
        STATS = sb("bn_stats", [P, TILES, 6])
        MV = sb("mean_var", [P, TILES, 2])
        VE = sb("var_eps", [P, TILES])
        SD = sb("std", [P, TILES])
        RSTD = sb("rstd", [P, TILES])
        stage_w = [sb(f"stage_w{s}", [P, WCOLS]) for s in range(2)]
        WE = [[sb(f"we_{n}{s}", [P, WCOLS], F32R) for n in ("hi", "lo")] for s in range(4)]
        SG = [PT[:, s, :] for s in range(2)]
        HF = [PT[:, 2 + s, :] for s in range(2)]
        HR = [[sb(f"h_{n}{s}", [P, SEQ], F32R) for n in ("hi", "lo")] for s in range(4)]
        SSC = sb("stream_scale", [P, FFN_CHUNKS, 2])
        DSC = sb("down_scale", [P, DM])
        GWS = sb("router_stage", [P, CH, EXPERTS])
        GWT = [sb(f"router_{n}", [P, CH, EXPERTS], F32R) for n in ("hi", "lo")]
        EB = sb("router_bias", [P, EXPERTS])
        TIES = sb("ties", [P, EXPERTS, EXPERTS])
        TIEG = sb("ties_groups", [P, NGRP, NGRP])
        R = {n: sb(f"route_{n}", [P, TILES, EXPERTS]) for n in ("e", "s", "b", "v", "gm", "w", "c")}
        RG = {n: sb(f"rgrp_{n}", [P, TILES, NGRP, w]) for n, w in (("hi", 2), ("lo", 2), ("t1", 1), ("a", 1), ("b", 1), ("s", 1))}
        CMPS = [sb(f"cmp{j}", [P, EXPERTS, EXPERTS]) for j in range(2)]
        RK = sb("rank", [P, TILES, EXPERTS])
        RKG = sb("rank_g", [P, TILES, NGRP])
        CG = sb("cmp_g", [P, 2, TILES, NGRP, NGRP])
        WSUM = sb("wsum", [P, TILES])
        WREC = sb("wrec", [P, TILES])

        PS = ctx.enter_context(nc.psum_tensor("psum", [P, 8, 512], F32))

        x_in, rows_in, tables_in = sem("x_in"), sem("rows_in"), sem("tables_in")
        wqkv_in, wo_in = sem("wqkv_in"), sem("wo_in")
        stream_in = [sem(f"stream_in{s}") for s in range(2)]
        zeroed = sem("zeroed")
        consts_ready = sem("consts_ready")
        out_stored = sem("out_stored")
        dve_self = sem("dve_self")
        act_self = sem("act_self")
        pool_self = sem("pool_self")
        var_ready, std_ready, normed = sem("var_ready"), sem("std_ready"), sem("normed")
        xT_ready, xT_hi_done, xT_lo_done = sem("xT_ready"), sem("xT_hi_done"), sem("xT_lo_done")
        wsplit_hi, wsplit_lo = sem("wsplit_hi"), sem("wsplit_lo")
        bias_added = sem("bias_added")
        proj_out_ready, resid_done = sem("proj_out_ready"), sem("resid_done")
        qkv_ready, qkv_taken = sem("qkv_ready"), sem("qkv_taken")
        rope_part, rope_done = sem("rope_part"), sem("rope_done")
        stack_hi, stack_lo = sem("stack_hi"), sem("stack_lo")
        v_stacked = sem("v_stacked")
        qT_ready, qT_taken = sem("qT_ready"), sem("qT_taken")
        kT_ready, kT_taken = sem("kT_ready"), sem("kT_taken")
        s1_ready, s1_reduced = sem("s1_ready"), sem("s1_reduced")
        m_hi, m_lo = sem("m_hi"), sem("m_lo")
        mT_ready, mT_taken = sem("mT_ready"), sem("mT_taken")
        s2_ready, exp_done = sem("s2_ready"), sem("exp_done")
        pv_done, o_taken = sem("pv_done"), sem("o_taken")
        oT_ready, rd_done, ctx_done = sem("oT_ready"), sem("rd_done"), sem("ctx_done")
        we_hi, we_lo = sem("we_hi"), sem("we_lo")
        gu_ready, silu_done, h_done = sem("gu_ready"), sem("silu_done"), sem("h_done")
        h_hi, h_lo = sem("h_hi"), sem("h_lo")
        y_ready, y_added = sem("y_ready"), sem("y_added")
        logits_ready, router_exp, routed = sem("logits_ready"), sem("router_exp"), sem("routed")
        out_scaled, out_ready = sem("out_scaled"), sem("out_ready")

        block = ctx.enter_context(nc.Block())

        def need(eng, s, value):
            if not isinstance(value, int) or value > 0:
                eng.wait_ge(s, value)

        class Steps:

            def __init__(self, s):
                self.s, self.n = s, 0

            def done(self, ins):
                self.n += 1
                return ins.then_inc(self.s, 1)

        def in_layer(c, d):
            return 0 <= c + d < GROUPS

        @block.sync
        def _(sp):
            def load(dst, src, s):
                sp.dma_start(dst, src).then_inc(s, 16)

            for t in range(0, TILES, 4):
                load(X[:, t:t + 4, :], x[:, t:t + 4, :], x_in)
            load(stage_qkv[:, :, :], wqkv[0], wqkv_in)
            load(BQKV[:, :], bqkv[0].partition_broadcast(P), rows_in)
            load(BO[:, :], bo[0].partition_broadcast(P), rows_in)
            load(ident[:, :], ident_in, tables_in)
            load(ROPE[:, :, :, :], rope, tables_in)
            load(mask_in[:, :, :], masks, tables_in)
            load(stage_wo[:, :, :], wo[0], wo_in)
            load(GWS[:, :, :], router_w, tables_in)
            load(EB[:, :], router_b.partition_broadcast(P), tables_in)
            load(TIES[:, :, :].rearrange("p a b -> p (a b)"), ties[0:1, 0:256].rearrange("a b -> (a b)").partition_broadcast(P), tables_in)
            load(TIEG[:, :, :].rearrange("p a b -> p (a b)"), ties[0:1, 256:272].rearrange("a b -> (a b)").partition_broadcast(P), tables_in)
            load(SSC[:, :, :], stream_scale, tables_in)
            load(DSC[:, :], down_scale.partition_broadcast(P), tables_in)
            for e in range(2):
                load(stage_w[e][:, :], stream_w[e], stream_in[e])
            need(sp, wsplit_lo, 1)
            load(stage_qkv[:, :, :], wqkv[1], wqkv_in)
            need(sp, wsplit_lo, 2)
            load(stage_wo[:, :, :], wo[1], wo_in)
            need(sp, qkv_taken, 4 * GROUPS)
            load(BQKV[:, :], bqkv[1].partition_broadcast(P), rows_in)
            need(sp, bias_added, 1)
            load(BO[:, :], bo[1].partition_broadcast(P), rows_in)

            def load_expert(i, c):
                sp.wait_ge(we_hi, 4 * i + c - 1)
                sp.wait_ge(we_lo, 4 * i + c - 1)
                load(stage_w[c % 2][:, :], stream_w[ds(4 * i + c, 1)].rearrange("e p w -> (e p) w"), stream_in[c % 2])

            with sp.Fori(0, 5) as i:
                for c in range(2, 6):
                    load_expert(i, c)
            load_expert(0, STREAM - 1)
            for t in range(TILES):
                sp.wait_ge(out_ready, t + 1)
                sp.dma_start(out[:, t, :], X[:, t, :]).then_inc(out_stored, 16)
            sp.wait_ge(out_stored, 16 * TILES)

        @block.tensor
        def _(pe):
            def product(dst, left, right, start=True, stop=True):
                pe.matmul(dst, left[0], right[0], start=start, stop=False)
                pe.matmul(dst, left[0], right[1], start=False, stop=False)
                return pe.matmul(dst, left[1], right[0], start=False, stop=stop)

            def to_features(norm=None, groups=None):
                if groups:
                    pe.wait_ge(ctx_done, groups)
                for f in range(2 * CH):
                    half, c = f // CH, f % CH
                    if c == 0 and not groups:
                        pe.wait_ge(normed, 2 * norm + half + 1)
                    for t in range(TPB):
                        mm = pe.transpose(PS[:, f, t * P:(t + 1) * P],
                                          XN[:, half * TPB + t, c * P:(c + 1) * P], ident[:, :])
                    mm.then_inc(xT_ready, 1)

            def project_out(layer):
                pe.wait_ge(xT_hi_done, 4 * (3 * layer + 2))
                pe.wait_ge(xT_lo_done, 4 * (3 * layer + 2))
                pe.wait_ge(wsplit_lo, 2 * layer + 2)
                for t in range(TILES):
                    need(pe, resid_done, TILES * layer + t - 3 if t >= 4 else 0)
                    for c in range(CH):
                        mm = product(PS[:, 4 + t % 4, 0:DM], [w[:, c, t * P:(t + 1) * P] for w in XT],
                                     [w[:, c, :] for w in WO], start=(c == 0), stop=(c == CH - 1))
                    mm.then_inc(proj_out_ready, 1)

            def transposes_v1(m, s, p):
                pe.wait_ge(stack_lo, 3 * m + 3)
                if p == 0:
                    need(pe, mT_taken, 2 * m - 1)
                    b = 0
                else:
                    pe.wait_ge(kT_taken, 4 * m + 2)
                    b = 1
                bank = BANK_T[(b + s) % 2]
                for t in range(TPB):
                    mm = pe.transpose(PS[:, bank, t * P:(t + 1) * P],
                                      QS[s][:, t * HPG + 2 * p:t * HPG + 2 * p + 2, :].bitcast(F32).rearrange("p h w -> p (h w)"), ident[:, :])
                mm.then_inc(qT_ready, 1)

            def transposes_k(m, s, p, had_o):
                if p == 0:
                    need(pe, mT_taken, 2 * m)
                    b = 1
                else:
                    if had_o:
                        pe.wait_ge(ctx_done, m - 1)
                    pe.wait_ge(qT_taken, 2 * m + 1)
                    b = 0
                bank = BANK_T[(b + s) % 2]
                for t in range(TPB):
                    mm = pe.transpose(PS[:, bank, t * P:(t + 1) * P],
                                      KS[s][:, t * HPG + 2 * p:t * HPG + 2 * p + 2, :].bitcast(F32).rearrange("p h w -> p (h w)"), ident[:, :])
                mm.then_inc(kT_ready, 1)

            def transposes_max(m, s, p):
                pe.wait_ge(m_lo, 2 * m + p + 1)
                if p == 0:
                    pe.wait_ge(qT_taken, 2 * m + 2)
                    b = 1
                else:
                    pe.wait_ge(kT_taken, 4 * m + 4)
                    b = 0
                bank = BANK_T[(b + s) % 2]
                for t in range(TPB):
                    mm = pe.transpose(PS[:, bank, t * P:(t + 1) * P],
                                      QS[s][:, t * HPG + 2 * p:t * HPG + 2 * p + 2, :].bitcast(F32).rearrange("p h w -> p (h w)"), ident[:, :])
                mm.then_inc(mT_ready, 1)

            def transposes_out(m, s):
                pe.wait_ge(o_taken, m + 1)
                return BANK_T[s % 2]

            def attention_step(layer, m, c):
                s0, s1 = c % 2, (c + 1) % 2
                has_c, has_b, has_a, has_o = (in_layer(c, d) for d in (0, 1, 2, -1))

                def project(unit):
                    g = m + 2
                    need(pe, qkv_taken, 4 * g + 2 * unit)
                    if unit == 0:
                        pe.wait_ge(xT_lo_done, 4 * (3 * layer + 1))
                        pe.wait_ge(xT_hi_done, 4 * (3 * layer + 1))
                        pe.wait_ge(wsplit_lo, 2 * layer + 1)
                    col = GW * ((g - GROUPS * layer) // 2) if isinstance(g, int) else (c + 2) // 2 * GW + (m - c - GROUPS * layer) * (GW // 2)
                    for j in range(2):
                        t = 4 * s0 + 2 * unit + j
                        for k in range(CH):
                            mm = product(PS[:, BANK_P, j * GW:(j + 1) * GW],
                                         [w[:, k, t * P:(t + 1) * P] for w in XT],
                                         [w[:, k, ds(col, GW)] for w in WQKV], start=(k == 0), stop=(k == CH - 1))
                    mm.then_inc(qkv_ready, 1)

                def scores(u):
                    g, h, qt = m + 1, u // TPB, u % TPB
                    keys = P * (qt + 1) if layer else SEQ
                    if u in (0, 8):
                        pe.wait_ge(qT_taken, 2 * g + u // 8 + 1)
                        pe.wait_ge(kT_taken, 4 * g + u // 4 + 2)
                    need(pe, s1_reduced, 16 * g + u - 1)
                    bank = BANK_S1[u % 2]
                    mm = pe.matmul(PS[:, bank, 0:keys], QT[s1][:, h // 2, qt * P:(qt + 1) * P],
                                   KT[s1][:, h, 0:keys], start=True, stop=(layer == 0))
                    if layer:
                        mm = pe.matmul(PS[:, bank, keys - P:keys], ident_r[:, :], mask_r[:, 0, :],
                                       start=False, stop=True)
                    mm.then_inc(s1_ready, 1)

                def scores_t(u):
                    kt, h = u // HPG, u % HPG
                    q0 = P * kt if layer else 0
                    if u == 0:
                        pe.wait_ge(mT_taken, 2 * m + 2)
                    if u >= 2:
                        pe.wait_ge(exp_done, 16 * m + u - 1)
                    bank = BANK_S2[u % 2]
                    mm = pe.matmul(PS[:, bank, q0:SEQ], KT[s0][:, h, kt * P:(kt + 1) * P],
                                   QT[s0][:, h // 2, q0:SEQ], start=True, stop=(layer == 0))
                    if layer:
                        mm = pe.matmul(PS[:, bank, q0:q0 + P], ident_r[:, :], mask_r[:, 1, :],
                                       start=False, stop=True)
                    mm.then_inc(s2_ready, 1)

                def values(kt):
                    q0 = P * kt if layer else 0
                    pe.wait_ge(exp_done, 16 * m + 4 * kt + 4)
                    if kt == 0:
                        need(pe, o_taken, m)
                        pe.wait_ge(v_stacked, m + 1)
                    for h in range(HPG):
                        mm = pe.matmul(PS[32 * h:32 * h + 32, BANK_O, q0:SEQ], VS[s0][:, kt, h, :],
                                       PT[:, (4 * kt + h) % NRING, q0:SEQ], start=(kt == 0),
                                       stop=(kt == TPB - 1), skip_group_check=True)
                    mm.then_inc(pv_done, 1)

                if has_b:
                    transposes_v1(m + 1, s1, 0)
                    transposes_k(m + 1, s1, 0, False)
                if has_a:
                    project(0)
                for j in range(TPB):
                    if j == 1:
                        if has_o:
                            pe.wait_ge(o_taken, m)
                            if has_b:
                                pe.wait_ge(qT_taken, 2 * (m + 1) + 1)
                            else:
                                pe.wait_ge(mT_taken, 2 * (m + 1) - 1)
                            for t in range(TPB):
                                mm = pe.transpose(PS[:, BANK_T[s1], t * P:(t + 1) * P],
                                                  OS[:, t * P:(t + 1) * P], ident[:, :])
                            mm.then_inc(oT_ready, 1)
                        if has_b:
                            transposes_v1(m + 1, s1, 1)
                            transposes_k(m + 1, s1, 1, has_o)
                        if has_a:
                            project(1)
                    if j == 3 and has_b:
                        transposes_max(m + 1, s1, 0)
                    for u in range(4 * j, 4 * j + 4):
                        if has_c:
                            scores_t(u)
                        if has_b:
                            scores(u)
                    if has_c and j >= 1:
                        values(j - 1)
                if has_c:
                    values(TPB - 1)
                if has_b:
                    transposes_max(m + 1, s1, 1)

            def attention(layer):
                base = GROUPS * layer
                for c in range(-2, GROUPS):
                    attention_step(layer, base + c, c)
                pe.wait_ge(o_taken, base + GROUPS)
                for t in range(TPB):
                    mm = pe.transpose(PS[:, BANK_T[0], t * P:(t + 1) * P], OS[:, t * P:(t + 1) * P], ident[:, :])
                mm.then_inc(oT_ready, 1)

            def gate_up(i, c, half):
                e = 4 * i + c
                k = 2 * e + half
                if half == 0:
                    pe.wait_ge(we_lo, e + 1)
                need(pe, h_done, k - 1 if not isinstance(k, int) or k >= 2 else 0)
                W = WE[c % 4]
                for bank, w0 in ((BANK_G[half], 0), (BANK_U[half], CH * P)):
                    for j in range(CH):
                        mm = product(PS[:, bank, :], [w[:, w0 + j * P:w0 + (j + 1) * P] for w in W],
                                     [w[:, j, half * SEQ:(half + 1) * SEQ] for w in XT],
                                     start=(j == 0), stop=(j == CH - 1))
                mm.then_inc(gu_ready, 1)

            def down(i, c, half):
                k = 8 * i + 2 * c + half
                pe.wait_ge(h_lo, k + 1)
                W, H = WE[c % 4], HR[(2 * c + half) % 4]
                for t in range(TPB):
                    need(pe, y_added, 4 * k + t - 3 if not isinstance(k, int) or k else 0)
                    product(PS[:, BANK_Y[t], 0:DM], [w[:, t * P:(t + 1) * P] for w in H],
                            [w[:, 2 * CH * P:] for w in W]).then_inc(y_ready, 1)

            def router():
                for t in range(TILES):
                    for c in range(CH):
                        mm = product(PS[:, 7, t * EXPERTS:(t + 1) * EXPERTS],
                                     [w[:, c, t * P:(t + 1) * P] for w in XT],
                                     [w[:, c, :] for w in GWT], start=(c == 0), stop=(c == CH - 1))
                mm.then_inc(logits_ready, 1)

            def units(pairs):
                for i, c in pairs:
                    for half in range(2):
                        gate_up(i, c, half)
                        down(i, c - 1, half)

            pe.wait_ge(consts_ready, 5)
            for layer in range(2):
                to_features(norm=2 * layer)
                attention(layer)
                to_features(groups=GROUPS * (layer + 1))
                project_out(layer)
                to_features(norm=2 * layer + 1)
                pe.wait_ge(xT_hi_done, 4 * (3 * layer + 3))
                pe.wait_ge(xT_lo_done, 4 * (3 * layer + 3))
                if layer == 0:
                    router()
                    for half in range(2):
                        gate_up(0, 0, half)
                    pe.wait_ge(router_exp, 1)
                    units([(0, 1)])
                    with pe.Fori(0, 3) as i:
                        units((i, c) for c in range(2, 6))
                    units((0, c) for c in range(14, 1 + EXPERTS))
                    for half in range(2):
                        down(0, EXPERTS, half)
                else:
                    for half in range(2):
                        gate_up(0, 17, half)
                    units((0, c) for c in range(18, STREAM))
                    for half in range(2):
                        down(0, STREAM - 1, half)

        @block.vector
        def _(dve):
            own = Steps(dve_self)

            def after_own():
                dve.wait_ge(dve_self, own.n)

            def layer_norm(l, ready):
                for t in range(TILES):
                    ready(t)
                    own.done(dve.bn_stats(STATS[:, t, :], X[:, t, :]))
                after_own()
                for t in range(TILES):
                    own.done(dve.bn_aggr(MV[:, t, :], STATS[:, t, :]))
                after_own()
                dve.tensor_scalar(VE[:, :], MV[:, :, 1], EPS, None, ALU.add).then_inc(var_ready, 1)
                dve.wait_ge(std_ready, l + 1)
                own.done(dve.reciprocal(RSTD[:, :], SD[:, :]))
                after_own()
                for t in range(TILES):
                    ins = dve.tensor_scalar(XN[:, t, :], X[:, t, :], MV[:, t, 0:1], RSTD[:, t:t + 1],
                                            ALU.subtract, ALU.mult)
                    if t % TPB == TPB - 1:
                        ins.then_inc(normed, 1)

            def to_features(l):
                for f in range(2 * CH):
                    half, c = f // CH, f % CH
                    dve.wait_ge(xT_hi_done, 4 * l + f + 1)
                    cols = slice(half * SEQ, (half + 1) * SEQ)
                    dve.tensor_tensor(XT[1][:, c, cols], PS[:, f, :], XT[0][:, c, cols].bitcast(F32),
                                      ALU.subtract).then_inc(xT_lo_done, 1)

            def attention_step(layer, m, c):
                s0, s1 = c % 2, (c + 1) % 2
                has_c, has_b, has_a, has_o = (in_layer(c, d) for d in (0, 1, 2, -1))

                def take_qkv(unit):
                    g = m + 2
                    dve.wait_ge(qkv_ready, 2 * g + unit + 1)
                    if unit == 0:
                        need(dve, stack_lo, 3 * g - 3)
                        need(dve, stack_hi, 2 * g - 2)
                        need(dve, v_stacked, g - 1)
                        if layer == 0:
                            need(dve, rope_part, 3 * g - 3)
                    if c == -2 and unit == 0:
                        dve.wait_ge(rows_in, 32 * (layer + 1))
                        dve.wait_ge(zeroed, 1)
                    col = GW * ((g - GROUPS * layer) // 2) if isinstance(g, int) else (c + 2) // 2 * GW + (m - c - GROUPS * layer) * (GW // 2)
                    got = PS[:, BANK_P, 0:2 * GW].rearrange("p (t w) -> p t w", t=2)
                    rows = slice(2 * HPG * unit, 2 * HPG * (unit + 1))
                    qk = QK[s0][:, :, rows, :].rearrange("p a (t h) d -> p a t (h d)", t=2)
                    for a in range(2):
                        bias = BQKV[:, ds(col + a * 64, 64)].unsqueeze(1).broadcast_to([P, 2, 64])
                        ins = dve.tensor_tensor(qk[:, a], got[:, :, a * 64:(a + 1) * 64], bias, ALU.add)
                    ins.then_inc(qkv_taken, 1)
                    vbias = BQKV[:, ds(col + 128, 64)].unsqueeze(1).broadcast_to([P, 2, 64])
                    dve.tensor_tensor(VR[s0][:, 2 * unit:2 * unit + 2, :], got[:, :, 128:192], vbias,
                                      ALU.add).then_inc(qkv_taken, 1)

                def take_qT(p):
                    g = m + 1
                    dve.wait_ge(qT_ready, 2 * g + p + 1)
                    if p == 0:
                        need(dve, s2_ready, 16 * g - 16)
                    bank = BANK_T[(p + s1) % 2]
                    dve.tensor_copy(QT[s1][:, p, :], PS[:, bank, :]).then_inc(qT_taken, 1)

                def reduce(u):
                    g, h, qt = m + 1, u // TPB, u % TPB
                    keys = P * (qt + 1) if layer else SEQ
                    dve.wait_ge(s1_ready, 16 * g + u + 1)
                    dve.tensor_reduce(MX[s1][:, h, qt:qt + 1], PS[:, BANK_S1[u % 2], 0:keys], AX.X,
                                      ALU.max).then_inc(s1_reduced, 1)

                def split_max(p):
                    g = m + 1
                    dve.wait_ge(s1_reduced, 16 * g + 8 * p + 8)
                    stack = QS[s1][:, :, :].rearrange("p (t h) w -> p t h w", t=TPB)
                    mx = MX[s1][:, 2 * p:2 * p + 2, :].rearrange("p h t -> p t h")
                    hi = stack[:, :, 2 * p:2 * p + 2, 3 * HD]
                    lo = stack[:, :, 2 * p:2 * p + 2, 3 * HD + 1]
                    dve.tensor_scalar(hi, mx, -1.0, None, ALU.mult).then_inc(m_hi, 1)
                    dve.wait_ge(m_hi, 2 * g + p + 1)
                    dve.scalar_tensor_tensor(lo, mx, -1.0, hi.bitcast(F32), ALU.mult,
                                             ALU.subtract).then_inc(m_lo, 1)

                if has_b:
                    take_qT(0)
                if has_o:
                    dve.wait_ge(pv_done, 4 * m)
                    need(dve, oT_ready, m - 1)
                    dve.tensor_copy(OS[:, :], PS[:, BANK_O, :]).then_inc(o_taken, 1)
                if has_a:
                    take_qkv(0)
                for j in range(TPB):
                    if j == 1:
                        if has_o:
                            normalise_context(layer, m - 1, c - 1, s1)
                        if has_b:
                            take_qT(1)
                        if has_a:
                            take_qkv(1)
                    if has_b:
                        for u in range(4 * j, 4 * j + 4):
                            reduce(u)
                    if j == 2 and has_b:
                        split_max(0)
                if has_b:
                    split_max(1)

            def normalise_context(layer, m, c, bank):
                T = PS[:, BANK_T[bank], :].rearrange("p (r w) -> p r w", w=32)
                dve.wait_ge(oT_ready, m + 1)
                dve.reciprocal(RD[:, :], T[:, :, HD]).then_inc(rd_done, 1)
                dve.wait_ge(rd_done, m + 1)
                t0 = TPB * (c % 2)
                col = HPG * HD * (c // 2) if isinstance(m, int) else (m - c - GROUPS * layer) * (HPG * HD // 2) + c // 2 * HPG * HD
                dst = XN[:, t0:t0 + TPB, ds(col, HPG * HD)].rearrange("p t (h d) -> p t h d", h=HPG)
                src = T[:, :, 0:HD].rearrange("p (t h) d -> p t h d", t=TPB)
                rd = RD[:, :].rearrange("p (t h) -> p t h", t=TPB).unsqueeze(3).broadcast_to([P, TPB, HPG, HD])
                dve.tensor_tensor(dst, src, rd, ALU.mult).then_inc(ctx_done, 1)

            def attention(layer):
                base = GROUPS * layer
                for c in range(-2, GROUPS):
                    attention_step(layer, base + c, c)
                dve.wait_ge(pv_done, 4 * (base + GROUPS))
                dve.wait_ge(oT_ready, base + GROUPS - 1)
                dve.tensor_copy(OS[:, :], PS[:, BANK_O, :]).then_inc(o_taken, 1)
                normalise_context(layer, base + GROUPS - 1, GROUPS - 1, 0)

            def residual(layer):
                def ready(t):
                    dve.wait_ge(proj_out_ready, TILES * layer + t + 1)
                    if t == 0:
                        dve.wait_ge(bias_added, layer + 1)
                    dve.tensor_tensor(X[:, t, :], PS[:, 4 + t % 4, 0:DM], X[:, t, :],
                                      ALU.add).then_inc(resid_done, 1)
                    dve.wait_ge(resid_done, TILES * layer + t + 1)
                return ready

            def router():
                def step(ins):
                    own.done(ins)
                    after_own()
                dve.wait_ge(router_exp, 1)
                step(dve.tensor_scalar(R["s"][:, :, :], R["e"][:, :, :], 1.0, None, ALU.add))
                step(dve.reciprocal(R["e"][:, :, :], R["s"][:, :, :]))
                sc = R["e"]
                step(dve.tensor_tensor(R["b"][:, :, :], sc[:, :, :],
                                       EB[:, :].unsqueeze(1).broadcast_to([P, TILES, EXPERTS]), ALU.add))
                b4 = R["b"][:, :, :].rearrange("p t (g a c) -> p (t g) a c", g=NGRP, a=2)
                fl = {n: v[:, :, :, :].rearrange("p t g w -> p (t g) w") for n, v in RG.items()}
                own.done(dve.tensor_tensor(fl["hi"][:, :, :], b4[:, :, :, 0], b4[:, :, :, 1], ALU.max))
                step(dve.tensor_tensor(fl["lo"][:, :, :], b4[:, :, :, 0], b4[:, :, :, 1], ALU.min))
                own.done(dve.tensor_tensor(fl["t1"][:, :, :], fl["hi"][:, :, 0:1], fl["hi"][:, :, 1:2], ALU.max))
                own.done(dve.tensor_tensor(fl["a"][:, :, :], fl["hi"][:, :, 0:1], fl["hi"][:, :, 1:2], ALU.min))
                step(dve.tensor_tensor(fl["b"][:, :, :], fl["lo"][:, :, 0:1], fl["lo"][:, :, 1:2], ALU.max))
                step(dve.tensor_tensor(fl["a"][:, :, :], fl["a"][:, :, :], fl["b"][:, :, :], ALU.max))
                step(dve.tensor_tensor(fl["s"][:, :, :], fl["t1"][:, :, :], fl["a"][:, :, :], ALU.add))
                gs = RG["s"][:, :, :, 0]
                mine = gs.unsqueeze(3).broadcast_to([P, TILES, NGRP, NGRP])
                other = gs.unsqueeze(2).broadcast_to([P, TILES, NGRP, NGRP])
                own.done(dve.tensor_tensor(CG[:, 0], other, mine, ALU.is_gt))
                step(dve.tensor_tensor(CG[:, 1], other, mine, ALU.is_equal))
                tg = TIEG[:, :, :].unsqueeze(1).broadcast_to([P, TILES, NGRP, NGRP])
                step(dve.tensor_tensor(CG[:, 1], CG[:, 1], tg, ALU.mult))
                step(dve.tensor_tensor(CG[:, 0], CG[:, 0], CG[:, 1], ALU.add))
                step(dve.tensor_reduce(RKG[:, :, :], CG[:, 0], AX.X, ALU.add))
                step(dve.tensor_scalar(RKG[:, :, :], RKG[:, :, :], float(2), None, ALU.is_lt))
                rk = RKG[:, :, :].unsqueeze(3).broadcast_to([P, TILES, NGRP, GSZ])
                v4 = R["v"][:, :, :].rearrange("p t (g c) -> p t g c", g=NGRP)
                b44 = R["b"][:, :, :].rearrange("p t (g c) -> p t g c", g=NGRP)
                g4 = R["gm"][:, :, :].rearrange("p t (g c) -> p t g c", g=NGRP)
                own.done(dve.tensor_scalar(g4, rk, 1.0, -NEG, ALU.subtract, ALU.mult))
                step(dve.tensor_tensor(v4, b44, rk, ALU.mult))
                step(dve.tensor_tensor(R["v"][:, :, :], R["v"][:, :, :], R["gm"][:, :, :], ALU.add))
                for t in range(TILES):
                    mine = R["v"][:, t, :].unsqueeze(2).broadcast_to([P, EXPERTS, EXPERTS])
                    other = R["v"][:, t, :].unsqueeze(1).broadcast_to([P, EXPERTS, EXPERTS])
                    own.done(dve.tensor_tensor(CMPS[0][:, :, :], other, mine, ALU.is_gt))
                    step(dve.tensor_tensor(CMPS[1][:, :, :], other, mine, ALU.is_equal))
                    step(dve.tensor_tensor(CMPS[1][:, :, :], CMPS[1][:, :, :], TIES[:, :, :], ALU.mult))
                    step(dve.tensor_tensor(CMPS[0][:, :, :], CMPS[0][:, :, :], CMPS[1][:, :, :], ALU.add))
                    step(dve.tensor_reduce(RK[:, t, :], CMPS[0][:, :, :], AX.X, ALU.add))
                step(dve.tensor_scalar(RK[:, :, :], RK[:, :, :], float(TOPK), None, ALU.is_lt))
                step(dve.tensor_tensor(R["w"][:, :, :], RK[:, :, :], sc[:, :, :], ALU.mult))
                step(dve.tensor_reduce(WSUM[:, :], R["w"][:, :, :], AX.X, ALU.add))
                step(dve.tensor_scalar(WSUM[:, :], WSUM[:, :], 1e-20, None, ALU.add))
                step(dve.reciprocal(WREC[:, :], WSUM[:, :]))
                step(dve.tensor_tensor(R["c"][:, :, :], R["w"][:, :, :],
                                       WREC[:, :].unsqueeze(2).broadcast_to([P, TILES, EXPERTS]), ALU.mult))
                dve.tensor_scalar(R["c"][:, :, :], R["c"][:, :, :], 2.5, None, ALU.mult).then_inc(routed, 1)
                dve.wait_ge(routed, 1)

            def hidden(i, c, half, ffn=None):
                k = 8 * i + 2 * c + half
                dve.wait_ge(silu_done, k + 1)
                need(dve, h_lo, k - 1 if not isinstance(k, int) or k >= 2 else 0)
                if ffn is None:
                    ins = dve.tensor_tensor(HF[half], PS[:, BANK_U[half], :], SG[half], ALU.mult)
                else:
                    ins = dve.scalar_tensor_tensor(HF[half], PS[:, BANK_U[half], :], SSC[:, ffn, 1:2],
                                                   SG[half], ALU.mult, ALU.mult)
                ins.then_inc(h_done, 1)

            def add_down(i, c, half, ffn=None):
                k = 8 * i + 2 * c + half
                for t in range(TPB):
                    dve.wait_ge(y_ready, 4 * k + t + 1)
                    tile = half * TPB + t
                    y = PS[:, BANK_Y[t], 0:DM]
                    need(dve, y_added, 4 * k + t - 7 if not isinstance(k, int) or 4 * k + t >= 8 else 0)
                    if ffn == 0:
                        ins = dve.tensor_copy(XN[:, tile, :], y)
                    elif ffn is not None:
                        ins = dve.tensor_tensor(XN[:, tile, :], y, XN[:, tile, :], ALU.add)
                    elif isinstance(i, int) and i == 0 and c == 0:
                        ins = dve.tensor_tensor(X[:, tile, :], y, X[:, tile, :], ALU.add)
                    else:
                        w = R["c"][:, tile, ds(4 * i + c - 1, 1)]
                        ins = dve.scalar_tensor_tensor(X[:, tile, :], y, w, X[:, tile, :],
                                                       ALU.mult, ALU.add)
                    ins.then_inc(y_added, 1)
                    if ffn == FFN_CHUNKS - 1:
                        dve.wait_ge(y_added, 4 * k + t + 1)
                        dve.tensor_tensor(XN[:, tile, :], XN[:, tile, :], DSC[:, :],
                                          ALU.mult).then_inc(out_scaled, 1)
                        dve.wait_ge(out_scaled, tile + 1)
                        dve.tensor_tensor(X[:, tile, :], X[:, tile, :], XN[:, tile, :],
                                          ALU.add).then_inc(out_ready, 1)

            dve.wait_ge(x_in, 32)
            for layer in range(2):
                if layer == 0:
                    layer_norm(0, lambda t: None)
                else:
                    dve.wait_ge(y_added, 8 * (1 + EXPERTS))
                    layer_norm(2, lambda t: None)
                to_features(3 * layer)
                attention(layer)
                to_features(3 * layer + 1)
                layer_norm(2 * layer + 1, residual(layer))
                to_features(3 * layer + 2)
                if layer == 0:
                    router()
                    for half in range(2):
                        hidden(0, 0, half)
                    for c in (1,):
                        for half in range(2):
                            hidden(0, c, half)
                            add_down(0, c - 1, half)
                    for c in range(2, 1 + EXPERTS):
                        for half in range(2):
                            hidden(0, c, half)
                            add_down(0, c - 1, half)
                    for half in range(2):
                        add_down(0, EXPERTS, half)
                else:
                    for half in range(2):
                        hidden(0, 17, half, 0)
                    for c in range(18, STREAM):
                        for half in range(2):
                            hidden(0, c, half, c - 17)
                            add_down(0, c - 1, half, c - 18)
                    for half in range(2):
                        add_down(0, STREAM - 1, half, FFN_CHUNKS - 1)

        @block.scalar
        def _(act):
            def root(l):
                act.wait_ge(var_ready, l + 1)
                act.activation(SD[:, :], VE[:, :], ACT.Sqrt).then_inc(std_ready, 1)

            def to_features(l):
                for f in range(2 * CH):
                    half, c = f // CH, f % CH
                    act.wait_ge(xT_ready, 4 * l + f + 1)
                    cols = slice(half * SEQ, (half + 1) * SEQ)
                    act.copy(XT[0][:, c, cols], PS[:, f, :]).then_inc(xT_hi_done, 1)

            def attention_step(layer, m, c):
                s0, s1 = c % 2, (c + 1) % 2
                has_c, has_b, has_a, has_o = (in_layer(c, d) for d in (0, 1, 2, -1))

                def take_kT(p):
                    g = m + 1
                    act.wait_ge(kT_ready, 2 * g + p + 1)
                    if p == 0:
                        need(act, s2_ready, 16 * g - 16)
                        need(act, zeroed, 1)
                    bank = BANK_T[(1 - p + s1) % 2]
                    for h in range(2):
                        rows = slice(64 * h, 64 * h + 64)
                        act.copy(KT[s1][rows, 2 * p + h, :], PS[rows, bank, :]).then_inc(kT_taken, 1)

                def take_mT(p):
                    act.wait_ge(mT_ready, 2 * (m + 1) + p + 1)
                    bank = BANK_T[(1 - p + s1) % 2]
                    act.copy(QT[s1][:, p, :], PS[:, bank, :]).then_inc(mT_taken, 1)

                def split_hi():
                    g = m + 2
                    src = QK[s0] if layer else ROPED[s0]
                    if layer:
                        act.wait_ge(qkv_taken, 4 * g + 4)
                    else:
                        act.wait_ge(rope_done, g + 1)
                    need(act, mT_ready, 2 * g - 2)
                    need(act, kT_ready, 2 * g - 2)
                    if c == -2:
                        act.wait_ge(zeroed, 1)
                    n = TPB * HPG
                    q2 = QS[s0][:, :, 0:2 * HD].rearrange("p r (a d) -> p r a d", a=2)
                    act.copy(q2, src[:, 0].unsqueeze(2).broadcast_to([P, n, 2, HD])).then_inc(stack_hi, 1)
                    k2 = KS[s0][:, :, :].rearrange("p r (a b d) -> p r a b d", a=2, b=2)[:, :, :, 0, :]
                    act.copy(k2, src[:, 1].unsqueeze(2).broadcast_to([P, n, 2, HD])).then_inc(stack_hi, 1)

                def exponentials(u):
                    kt = u // HPG
                    q0 = P * kt if layer else 0
                    act.wait_ge(s2_ready, 16 * m + u + 1)
                    act.activation(PT[:, u % NRING, q0:SEQ], PS[:, BANK_S2[u % 2], q0:SEQ], ACT.Exp,
                                   scale=SCALE).then_inc(exp_done, 1)

                if has_b:
                    take_kT(0)
                for j in range(TPB):
                    if j == 1 and has_b:
                        take_kT(1)
                    if has_c:
                        for u in range(4 * j, 4 * j + 4):
                            exponentials(u)
                    if j == 2 and has_a:
                        split_hi()
                    if j == 3 and has_b:
                        take_mT(0)
                if has_b:
                    take_mT(1)

            def attention(layer):
                for c in range(-2, GROUPS):
                    attention_step(layer, GROUPS * layer + c, c)

            def split_weights(n):
                dst, src, s = ((WQKV, stage_qkv, wqkv_in), (WO, stage_wo, wo_in))[n % 2]
                act.wait_ge(s, 16 * (n // 2 + 1))
                act.copy(dst[0][:, :, :], src[:, :, :]).then_inc(wsplit_hi, 1)

            def split_expert(i, c):
                e = 4 * i + c
                act.wait_ge(stream_in[c % 2], 32 * i + 16 * (c // 2 + 1))
                need(act, y_ready, 8 * (e - 3) if not isinstance(e, int) or e >= 4 else 0)
                act.copy(WE[c % 4][0][:, :], stage_w[c % 2][:, :]).then_inc(we_hi, 1)

            def unit(i, c, half, ffn=None):
                k = 8 * i + 2 * c + half
                act.wait_ge(gu_ready, k + 1)
                need(act, h_done, k - 1 if not isinstance(k, int) or k >= 2 else 0)
                act.activation(SG[half], PS[:, BANK_G[half], :], ACT.Silu,
                               scale=1.0 if ffn is None else SSC[:, ffn, 0:1]).then_inc(silu_done, 1)
                act.wait_ge(h_done, k + 1)
                need(act, y_ready, 4 * (k - 3) if not isinstance(k, int) or k >= 4 else 0)
                act.copy(HR[(2 * c + half) % 4][0][:, :], HF[half]).then_inc(h_hi, 1)

            act.wait_ge(tables_in, 16 * 9)
            act.copy(ident_r[:, :], ident[:, :]).then_inc(consts_ready, 1)
            act.copy(mask_r[:, :, :], mask_in[:, :, :]).then_inc(consts_ready, 1)
            act.copy(GWT[0][:, :, :], GWS[:, :, :]).then_inc(consts_ready, 1)
            for layer in range(2):
                if layer == 0:
                    root(0)
                    split_weights(0)
                    split_weights(1)
                else:
                    root(2)
                to_features(3 * layer)
                attention(layer)
                to_features(3 * layer + 1)
                root(2 * layer + 1)
                to_features(3 * layer + 2)
                if layer == 0:
                    act.wait_ge(logits_ready, 1)
                    act.activation(R["e"][:, :, :].rearrange("p t e -> p (t e)"),
                                   PS[:, 7, 0:TILES * EXPERTS], ACT.Exp, scale=-1.0).then_inc(router_exp, 1)
                    split_expert(0, 0)
                    split_expert(0, 1)
                    for half in range(2):
                        unit(0, 0, half)
                        if half == 0:
                            split_expert(0, 2)
                    for c in range(1, 1 + EXPERTS):
                        for half in range(2):
                            unit(0, c, half)
                            if half == 0:
                                split_expert(0, c + 2)
                    split_weights(2)
                    split_weights(3)
                else:
                    for c in range(17, STREAM):
                        for half in range(2):
                            unit(0, c, half, c - 17)
                            if half == 0 and c + 2 < STREAM:
                                split_expert(0, c + 2)

        @block.gpsimd
        def _(pool):
            own = Steps(pool_self)
            for s in range(2):
                own.done(pool.memset(QS[s][:, :, :].bitcast(F32), 0.0))
                own.done(pool.memset(KS[s][:, :, :].bitcast(F32), 0.0))
                own.done(pool.memset(KT[s][:, :, :].bitcast(F32), 0.0))
                own.done(pool.memset(VS[s][:, :, :, :], 0.0))
            pool.wait_ge(pool_self, own.n)
            for s in range(2):
                own.done(pool.memset(KS[s][:, :, 3 * HD:3 * HD + 2].bitcast(F32), 1.0))
                own.done(pool.memset(VS[s][:, :, :, HD:HD + 1], 1.0))
            pool.wait_ge(pool_self, own.n)
            pool.memset(RD[:, :], 0.0).then_inc(zeroed, 1)

            def split_weights(n):
                dst, src = ((WQKV, stage_qkv), (WO, stage_wo))[n % 2]
                pool.wait_ge(wsplit_hi, n + 1)
                pool.tensor_tensor(dst[1][:, :, :], src[:, :, :], dst[0][:, :, :].bitcast(F32),
                                   ALU.subtract).then_inc(wsplit_lo, 1)

            def split_expert(i, c):
                pool.wait_ge(we_hi, 4 * i + c + 1)
                pool.tensor_tensor(WE[c % 4][1][:, :], stage_w[c % 2][:, :],
                                   WE[c % 4][0][:, :].bitcast(F32), ALU.subtract).then_inc(we_lo, 1)

            def attention_step(layer, m, c):
                if in_layer(c, 1):
                    s1 = (c + 1) % 2
                    pool.wait_ge(qkv_taken, 4 * m + 8)
                    need(pool, pv_done, 4 * m)
                    pool.tensor_copy(VS[s1][:, :, :, 0:HD],
                                     VR[s1][:, :, :].rearrange("p t (h d) -> p t h d", h=HPG)).then_inc(v_stacked, 1)
                if not in_layer(c, 2):
                    return
                g, s0 = m + 2, c % 2
                if layer == 0:
                    pool.wait_ge(qkv_taken, 4 * g + 4)
                    need(pool, rope_done, g)
                    need(pool, stack_hi, 2 * g - 2)
                    half = TPB * HPG
                    cos = ROPE[:, 0].rearrange("p r d -> p (r d)").unsqueeze(1).broadcast_to([P, 2, half * HD])
                    pool.tensor_tensor(ROPED[s0][:, :, :, :].rearrange("p a r d -> p a (r d)"),
                                       QK[s0][:, :, :, :].rearrange("p a r d -> p a (r d)"), cos,
                                       ALU.mult).then_inc(rope_part, 1)
                    for j in range(2):
                        d, o = slice(8 * j, 8 * j + 8), slice(8 - 8 * j, 16 - 8 * j)
                        sin = ROPE[:, 1, :, d].unsqueeze(1).broadcast_to([P, 2, half, 8])
                        pool.tensor_tensor(ROT[:, :, :, d], QK[s0][:, :, :, o], sin,
                                           ALU.mult).then_inc(rope_part, 1)
                    pool.wait_ge(rope_part, 3 * g + 3)
                    pool.tensor_tensor(ROPED[s0][:, :, :, :], ROPED[s0][:, :, :, :], ROT[:, :, :, :],
                                       ALU.add).then_inc(rope_done, 1)
                src = QK[s0] if layer else ROPED[s0]
                pool.wait_ge(stack_hi, 2 * g + 2)
                pool.memset(QS[s0][:, :, 3 * HD:3 * HD + 2].bitcast(F32), 0.0).then_inc(stack_lo, 1)
                pool.tensor_tensor(QS[s0][:, :, 2 * HD:3 * HD], src[:, 0],
                                   QS[s0][:, :, 0:HD].bitcast(F32), ALU.subtract).then_inc(stack_lo, 1)
                pool.tensor_tensor(KS[s0][:, :, HD:2 * HD], src[:, 1],
                                   KS[s0][:, :, 0:HD].bitcast(F32), ALU.subtract).then_inc(stack_lo, 1)

            def attention(layer):
                for c in range(-2, GROUPS):
                    attention_step(layer, GROUPS * layer + c, c)

            def unit(i, c, half):
                k = 8 * i + 2 * c + half
                pool.wait_ge(h_hi, k + 1)
                H = HR[(2 * c + half) % 4]
                pool.tensor_tensor(H[1][:, :], HF[half], H[0][:, :].bitcast(F32),
                                   ALU.subtract).then_inc(h_lo, 1)

            def add_bias(layer):
                pool.wait_ge(rows_in, 32 * (layer + 1))
                pool.wait_ge(normed, 4 * layer + 2)
                pool.tensor_tensor(X[:, :, :], X[:, :, :],
                                   BO[:, :].unsqueeze(1).broadcast_to([P, TILES, DM]),
                                   ALU.add).then_inc(bias_added, 1)

            pool.wait_ge(consts_ready, 3)
            pool.tensor_tensor(GWT[1][:, :, :], GWS[:, :, :], GWT[0][:, :, :].bitcast(F32),
                               ALU.subtract).then_inc(consts_ready, 2)
            for layer in range(2):
                if layer == 0:
                    split_weights(0)
                    split_weights(1)
                add_bias(layer)
                attention(layer)
                if layer == 0:
                    split_expert(0, 0)
                    split_expert(0, 1)
                    for half in range(2):
                        unit(0, 0, half)
                        if half == 0:
                            split_expert(0, 2)
                    for c in range(1, 1 + EXPERTS):
                        for half in range(2):
                            unit(0, c, half)
                            if half == 0:
                                split_expert(0, c + 2)
                    split_weights(2)
                    split_weights(3)
                else:
                    for c in range(17, STREAM):
                        for half in range(2):
                            unit(0, c, half)
                            if half == 0 and c + 2 < STREAM:
                                split_expert(0, c + 2)


def _chunks(w):
    return np.ascontiguousarray(w.reshape(-1, P, w.shape[1]).transpose(1, 0, 2))


def _by_group(w):
    lead = w.shape[:-1]
    w = w.reshape(*lead, 3, HEADS // HPG, HPG * HD)
    return np.ascontiguousarray(np.swapaxes(w, -3, -2)).reshape(*lead, 3 * DM)


def _stream(gate, up, down):
    g, u = (_chunks(w.T).reshape(P, CH * P) for w in (gate, up))
    return np.concatenate([g, u, down.T], axis=1)


def _rope_tables():
    inv = 1.0 / 10000.0 ** (np.arange(0, HD, 2, dtype=np.float32) / HD)
    freqs = np.outer(np.arange(SEQ, dtype=np.float32), inv)
    emb = np.concatenate([freqs, freqs], axis=-1)
    cos, sin = np.cos(emb).astype(np.float32), np.sin(emb).astype(np.float32)
    sin[:, :HD // 2] = -sin[:, :HD // 2]
    both = np.stack([cos, sin]).reshape(2, TPB, P, 1, HD)
    both = np.broadcast_to(both, (2, TPB, P, HPG, HD)).transpose(2, 0, 1, 3, 4)
    return np.ascontiguousarray(both).reshape(P, 2, TPB * HPG, HD)


def kernel(**inputs):
    import concourse.bacc as _bacc
    from concourse.bass_utils import run_bass_kernel_spmd as _run

    a = {k: np.asarray(v) for k, v in inputs.items()}
    tri = np.triu(np.ones((P, P), np.float32), 1) * np.float32(NEG)
    lower = [(np.arange(n)[None, :] < np.arange(n)[:, None]).astype(np.float32).ravel() for n in (EXPERTS, NGRP)]
    pad = FFN_CHUNKS * P - FFN_INTER
    gw, uw, dw = a["L1_ffn_gate_w"], a["L1_ffn_up_w"], a["L1_ffn_down_w"]
    gw, uw = (np.concatenate([w, np.zeros((pad, DM), np.float32)]) for w in (gw, uw))
    dw = np.concatenate([dw, np.zeros((DM, pad), np.float32)], axis=1)
    rows = [slice(c * P, (c + 1) * P) for c in range(FFN_CHUNKS)]
    stream = [_stream(a["L0_ffn_shared_gate"], a["L0_ffn_shared_up"], a["L0_ffn_shared_down"])]
    stream += [_stream(a["L0_ffn_gate_proj"][e], a["L0_ffn_up_proj"][e], a["L0_ffn_down_proj"][e]) for e in range(EXPERTS)]
    stream += [_stream(gw[r], uw[r], dw[:, r]) for r in rows]
    scales = [np.concatenate([a[n], np.zeros(pad, np.float32)]).reshape(FFN_CHUNKS, P).T for n in ("L1_ffn_gate_s", "L1_ffn_up_s")]
    w0 = np.concatenate([a["L0_attn_Wq"].T, a["L0_attn_Wk"].T, a["L0_attn_Wv"].T], axis=1)
    b0 = np.concatenate([a["L0_attn_bq"], a["L0_attn_bk"], a["L0_attn_bv"]])
    arrays = {
        "x": _chunks(a["L0_attn_x"].reshape(-1, DM)),
        "wqkv": np.stack([_chunks(_by_group(w0)), _chunks(_by_group(a["L1_attn_w_qkv"]))]),
        "bqkv": np.stack([_by_group(b0), _by_group(a["L1_attn_b_qkv"])]),
        "wo": np.stack([_chunks(a["L0_attn_Wo"].T), _chunks(a["L1_attn_w_proj"])]),
        "bo": np.stack([a["L0_attn_bo"], a["L1_attn_b_proj"]]),
        "rope": _rope_tables(),
        "masks": np.ascontiguousarray(np.stack([tri, tri.T], axis=1)),
        "ident": np.eye(P, dtype=np.float32),
        "router_w": _chunks(a["L0_ffn_gate_weight"].T),
        "router_b": a["L0_ffn_expert_bias"],
        "ties": np.concatenate(lower)[None],
        "stream_w": np.stack(stream),
        "stream_scale": np.ascontiguousarray(np.stack(scales, axis=2)),
        "down_scale": a["L1_ffn_down_s"],
    }
    nc = _bacc.Bacc("TRN2", target_bir_lowering=False, num_devices=1)
    args = [nc.dram_tensor(f"in_{n}", v.shape, F32, kind="ExternalInput").ap() for n, v in arrays.items()]
    args.append(nc.dram_tensor("out_0", (P, TILES, DM), F32, kind="ExternalOutput").ap())
    two_layers(nc, *args)
    r = _run(nc, [{f"in_{n}": v for n, v in arrays.items()}], core_ids=[0])
    got = np.asarray(r.results[0]["out_0"])
    return np.ascontiguousarray(got.transpose(1, 0, 2)).reshape(BATCH, SEQ, DM)
```

```python
from contextlib import ExitStack

import numpy as np

import concourse.bass as bass
from concourse import mybir

P = 128
BATCH, SEQ, DM = 2, 512, 256
TILES = BATCH * SEQ // P
TPB = SEQ // P
CH = DM // P
HEADS, HD = 16, 16
HPG = 4
GROUPS = BATCH * HEADS // HPG
GW = 3 * HPG * HD
SLOT = 64
EXPERTS, TOPK, INTER = 16, 4, 128
NGRP, GSZ = 4, 4
FFN_INTER = 704
FFN_CHUNKS = -(-FFN_INTER // P)
STREAM = 1 + EXPERTS + FFN_CHUNKS
WCOLS = 2 * CH * P + DM
SCALE = HD ** -0.5
EPS = 1e-5
NEG = -1e30

F32 = mybir.dt.float32
F32R = mybir.dt.float32r
BF16 = mybir.dt.bfloat16
ACT = mybir.ActivationFunctionType
ALU = mybir.AluOpType
AX = mybir.AxisListType
ds = bass.ds

BANK_S1, BANK_S2, BANK_O, BANK_T = (0, 1), (2, 3), 4, (5, 6, 7)
BANK_G, BANK_U, BANK_Y = (0, 1), (2, 3), (4, 5, 6, 7)
FILLS = ((0, 0), (0, 1), (1, 0), (1, 1))
BANK_NORM = (4, 6, 1, 3)
CTX_FILLS = ((0, 0), (1, 0), (0, 1), (1, 1))
BANK_CTX = (0, 1, 5, 6)
BANK_PROJ = (2, 3, 0, 1)
VALUES_AT = ((6, 9, 13), (6, 10, 15))
F67 = (13, 14)
BANK_LT, BANK_LOGITS = (4, 6), 5


def two_layers(nc, x, wqkv, bqkv, wo, bo, rope, mask, ident_in, router_w, router_b, ties, stream_w,
               stream_scale, down_scale, out):
    with ExitStack() as ctx:
        def sb(name, shape, dt=F32):
            return ctx.enter_context(nc.sbuf_tensor(name, shape, dt))

        def sem(name):
            return ctx.enter_context(nc.semaphore(name))

        X = sb("resid", [P, TILES, DM])
        XN = sb("normed", [P, TILES, DM])
        XT = [sb(f"xT_{n}", [P, CH, BATCH * SEQ], F32R) for n in ("hi", "lo")]
        stage_qkv = sb("stage_qkv", [P, CH, 3 * DM])
        WQKV = [sb(f"wqkv_{n}", [P, CH, 3 * DM], F32R) for n in ("hi", "lo")]
        stage_wo = sb("stage_wo", [P, CH, DM])
        WO = [sb(f"wo_{n}", [P, CH, DM], F32R) for n in ("hi", "lo")]
        BQKV = sb("b_qkv", [P, 3 * DM])
        BO = sb("b_o", [P, DM])
        ROPE = sb("rope_tables", [P, 2, TPB * HPG, HD])
        ident = sb("ident", [P, P])
        ident_r = sb("ident_r", [P, P], F32R)
        mask_in = sb("mask_in", [P, P])
        mask_r = sb("mask_r", [P, P], F32R)
        QKV = [sb(f"qkv{s}", [P, 3, TPB * HPG, HD]) for s in range(2)]
        QK = [q[:, 0:2] for q in QKV]
        ROT = sb("rotated", [P, 2, TPB * HPG, HD])
        ROPED = [sb(f"roped{s}", [P, 2, TPB * HPG, HD]) for s in range(2)]
        QS = [sb(f"q_stack{s}", [P, TPB * HPG, SLOT], F32R) for s in range(2)]
        KS = [sb(f"k_stack{s}", [P, TPB * HPG, SLOT], F32R) for s in range(2)]
        QT = [sb(f"qT{s}", [P, 2, SEQ], F32R) for s in range(2)]
        KT = [sb(f"kT{s}", [P, HPG, SEQ], F32R) for s in range(2)]
        VS = [sb(f"v_stack{s}", [P, TPB, HPG, 32]) for s in range(2)]
        NRING = 8
        PT = sb("probsT", [P, NRING, SEQ])
        OS = sb("outT", [P, SEQ])
        MX = [sb(f"maxes{s}", [P, HPG, TPB]) for s in range(2)]
        RD = sb("rdenom", [P, TPB * HPG])
        STATS = sb("bn_stats", [P, TILES, 6])
        MV = sb("mean_var", [P, TILES, 2])
        VE = sb("var_eps", [P, TILES])
        SD = sb("std", [P, TILES])
        RSTD = sb("rstd", [P, TILES])
        stage_w = [sb(f"stage_w{s}", [P, WCOLS]) for s in range(2)]
        WE = [[sb(f"we_{n}{s}", [P, WCOLS], F32R) for n in ("hi", "lo")] for s in range(4)]
        SG = [PT[:, s, :] for s in range(2)]
        HF = [PT[:, 2 + s, :] for s in range(2)]
        HR = [[sb(f"h_{n}{s}", [P, SEQ], F32R) for n in ("hi", "lo")] for s in range(4)]
        SSC = sb("stream_scale", [P, FFN_CHUNKS, 2])
        DSC = sb("down_scale", [P, DM])
        LT = PT[0:EXPERTS, 4:6, :]
        CMP = [PT[:, 2 * s + 4:2 * s + 6, :].bitcast(BF16).rearrange("p a (b c) -> p (a b) c", c=EXPERTS) for s in range(2)]
        TIEB = sb("ties_bf16", [P, EXPERTS, EXPERTS], BF16)
        GWS = sb("router_stage", [P, CH, EXPERTS])
        GWT = [sb(f"router_{n}", [P, CH, EXPERTS], F32R) for n in ("hi", "lo")]
        EB = sb("router_bias", [P, EXPERTS])
        TIES = sb("ties", [P, EXPERTS, EXPERTS])
        TIEG = sb("ties_groups", [P, NGRP, NGRP])
        R = {n: sb(f"route_{n}", [P, TILES, EXPERTS]) for n in ("e", "s", "b", "v", "gm", "w", "c")}
        RG = {n: sb(f"rgrp_{n}", [P, TILES, NGRP, w]) for n, w in (("hi", 2), ("lo", 2), ("t1", 1), ("a", 1), ("b", 1), ("s", 1))}
        RK = sb("rank", [P, TILES, EXPERTS])
        RKG = sb("rank_g", [P, TILES, NGRP])
        CG = sb("cmp_g", [P, 2, TILES, NGRP, NGRP])
        WSUM = sb("wsum", [P, TILES])
        WREC = sb("wrec", [P, TILES])

        PS = ctx.enter_context(nc.psum_tensor("psum", [P, 8, 512], F32))

        x_in = [sem(f"x_in{half}") for half in range(2)]
        rows_in, tables_in = sem("rows_in"), sem("tables_in")
        ident_loaded, rope_in = sem("ident_loaded"), sem("rope_in")
        ident_r_ready = sem("ident_r_ready")
        wqkv_in, wo_in = sem("wqkv_in"), sem("wo_in")
        stream_in = [sem(f"stream_in{s}") for s in range(2)]
        zeroed = sem("zeroed")
        consts_ready = sem("consts_ready")
        out_stored = sem("out_stored")
        dve_self = sem("dve_self")
        pool_self = sem("pool_self")
        var_ready, std_ready, normed = sem("var_ready"), sem("std_ready"), sem("normed")
        xT_ready, xT_hi_done, xT_lo_done = sem("xT_ready"), sem("xT_hi_done"), sem("xT_lo_done")
        wsplit_hi, wsplit_lo = sem("wsplit_hi"), sem("wsplit_lo")
        bias_added = sem("bias_added")
        proj_out_ready, resid_done = sem("proj_out_ready"), sem("resid_done")
        qkv_ready, qkv_taken = sem("qkv_ready"), sem("qkv_taken")
        rope_part, rope_done = sem("rope_part"), sem("rope_done")
        stack_hi, stack_lo = sem("stack_hi"), sem("stack_lo")
        v_stacked = sem("v_stacked")
        qT_ready, qT_taken = sem("qT_ready"), sem("qT_taken")
        kT_ready, kT_taken = sem("kT_ready"), sem("kT_taken")
        s1_ready, s1_reduced = sem("s1_ready"), sem("s1_reduced")
        m_hi, m_lo = sem("m_hi"), sem("m_lo")
        mT_ready, mT_taken = sem("mT_ready"), sem("mT_taken")
        s2_ready, exp_done, probs_masked = sem("s2_ready"), sem("exp_done"), sem("probs_masked")
        pv_done, o_taken = sem("pv_done"), sem("o_taken")
        oT_ready, rd_done, ctx_done = sem("oT_ready"), sem("rd_done"), sem("ctx_done")
        we_hi, we_lo = sem("we_hi"), sem("we_lo")
        gu_ready, silu_done, h_done = sem("gu_ready"), sem("silu_done"), sem("h_done")
        h_hi, h_lo = sem("h_hi"), sem("h_lo")
        y_ready, y_added = sem("y_ready"), sem("y_added")
        lT_ready, lT_taken = sem("logitsT_ready"), sem("logitsT_taken")
        logits_ready, router_exp, routed = sem("logits_ready"), sem("router_exp"), sem("routed")
        out_scaled, out_ready = sem("out_scaled"), sem("out_ready")

        block = ctx.enter_context(nc.Block())

        def need(eng, s, value):
            if not isinstance(value, int) or value > 0:
                eng.wait_ge(s, value)

        class Steps:

            def __init__(self, s):
                self.s, self.n = s, 0

            def done(self, ins):
                self.n += 1
                return ins.then_inc(self.s, 1)

        def in_layer(c, d):
            return 0 <= c + d < GROUPS

        def rope_cos(s, rows):
            width = (rows.stop - rows.start) * HD
            cos = ROPE[:, 0, rows, :].rearrange("p r d -> p (r d)").unsqueeze(1).broadcast_to([P, 2, width])
            flat = [w[:, :, rows, :].rearrange("p a r d -> p a (r d)") for w in (ROPED[s], QK[s])]
            return flat[0], flat[1], cos, ALU.mult

        def rope_sin(s, rows, j):
            d, o = slice(8 * j, 8 * j + 8), slice(8 - 8 * j, 16 - 8 * j)
            sin = ROPE[:, 1, rows, d].unsqueeze(1).broadcast_to([P, 2, rows.stop - rows.start, 8])
            return ROT[:, :, rows, d], QK[s][:, :, rows, o], sin, ALU.mult

        def rope_sum(s, rows):
            return ROPED[s][:, :, rows, :], ROPED[s][:, :, rows, :], ROT[:, :, rows, :], ALU.add

        def q_lo(layer, s):
            src = QK[s] if layer else ROPED[s]
            return QS[s][:, :, 2 * HD:3 * HD], src[:, 0], QS[s][:, :, 0:HD].bitcast(F32), ALU.subtract

        def k_lo(layer, s):
            src = QK[s] if layer else ROPED[s]
            return KS[s][:, :, HD:2 * HD], src[:, 1], KS[s][:, :, 0:HD].bitcast(F32), ALU.subtract

        @block.sync
        def _(sp):
            def load(dst, src, s):
                sp.dma_start(dst, src).then_inc(s, 16)

            load(ident[:, :], ident_in, ident_loaded)
            for t in range(0, TILES, TPB):
                load(X[:, t:t + 4, :], x[:, t:t + 4, :], x_in[t // TPB])
            load(stage_qkv[:, :, :], wqkv[0], wqkv_in)
            load(BQKV[:, :], bqkv[0].partition_broadcast(P), rows_in)
            load(BO[:, :], bo[0].partition_broadcast(P), rows_in)
            load(ROPE[:, :, :, :], rope, rope_in)
            load(stage_wo[:, :, :], wo[0], wo_in)
            load(mask_in[:, :], mask, tables_in)
            load(GWS[:, :, :], router_w, tables_in)
            load(EB[:, :], router_b.partition_broadcast(P), tables_in)
            load(TIES[:, :, :].rearrange("p a b -> p (a b)"), ties[0:1, 0:256].rearrange("a b -> (a b)").partition_broadcast(P), tables_in)
            load(TIEG[:, :, :].rearrange("p a b -> p (a b)"), ties[0:1, 256:272].rearrange("a b -> (a b)").partition_broadcast(P), tables_in)
            load(SSC[:, :, :], stream_scale, tables_in)
            load(DSC[:, :], down_scale.partition_broadcast(P), tables_in)
            for e in range(2):
                load(stage_w[e][:, :], stream_w[e], stream_in[e])
            need(sp, wsplit_lo, 1)
            load(stage_qkv[:, :, :], wqkv[1], wqkv_in)
            need(sp, wsplit_lo, 2)
            load(stage_wo[:, :, :], wo[1], wo_in)
            need(sp, qkv_taken, 4 * GROUPS)
            load(BQKV[:, :], bqkv[1].partition_broadcast(P), rows_in)
            need(sp, bias_added, 1)
            load(BO[:, :], bo[1].partition_broadcast(P), rows_in)

            def load_expert(i, c):
                sp.wait_ge(we_hi, 4 * i + c - 1)
                sp.wait_ge(we_lo, 4 * i + c - 1)
                load(stage_w[c % 2][:, :], stream_w[ds(4 * i + c, 1)].rearrange("e p w -> (e p) w"), stream_in[c % 2])

            with sp.Fori(0, 5) as i:
                for c in range(2, 6):
                    load_expert(i, c)
            load_expert(0, STREAM - 1)
            for t in range(TILES):
                sp.wait_ge(out_ready, t + 1)
                sp.dma_start(out[:, t, :], X[:, t, :]).then_inc(out_stored, 16)
            sp.wait_ge(out_stored, 16 * TILES)

        @block.tensor
        def _(pe):
            def product(dst, left, right, start=True, stop=True, skip=False):
                pe.matmul(dst, left[0], right[0], start=start, stop=False, skip_group_check=skip)
                pe.matmul(dst, left[0], right[1], start=False, stop=False, skip_group_check=skip)
                return pe.matmul(dst, left[1], right[0], start=False, stop=stop, skip_group_check=skip)

            def to_features(fill, bank):
                half, c = fill
                for t in range(TPB):
                    mm = pe.transpose(PS[:, bank, t * P:(t + 1) * P],
                                      XN[:, half * TPB + t, c * P:(c + 1) * P], ident[:, :])
                mm.then_inc(xT_ready, 1)

            def norm_to_features(l, half):
                pe.wait_ge(normed, 2 * l + half + 1)
                for c in range(CH):
                    to_features((half, c), BANK_NORM[2 * half + c])

            def context_to_features(layer, f):
                half, c = CTX_FILLS[f]
                pe.wait_ge(ctx_done, GROUPS * layer + (3, 4, 7, 8)[f])
                to_features((half, c), BANK_CTX[f])

            def features_there(n):
                pe.wait_ge(xT_hi_done, n)
                pe.wait_ge(xT_lo_done, n)

            def project_out(layer, t):
                if t % TPB == 0:
                    features_there(12 * layer + (7, 8)[t // TPB])
                    pe.wait_ge(wsplit_lo, 2 * layer + 2)
                need(pe, resid_done, TILES * layer + t - 3 if t >= 4 else 0)
                for c in range(CH):
                    mm = product(PS[:, BANK_PROJ[t % 4], 0:DM], [w[:, c, t * P:(t + 1) * P] for w in XT],
                                 [w[:, c, :] for w in WO], start=(c == 0), stop=(c == CH - 1))
                mm.then_inc(proj_out_ready, 1)

            def attention_step(layer, m, c):
                s0, s1 = c % 2, (c + 1) % 2
                has_c, has_b, has_a, has_o = (in_layer(c, d) for d in (0, 1, 2, -1))

                def project(unit, j):
                    g = m + 2
                    if j == 0 and unit == 0:
                        if has_b:
                            pe.wait_ge(qT_taken, 2 * m + 3)
                        features_there(12 * layer + (2 if c == -2 else 4))
                        pe.wait_ge(wsplit_lo, 2 * layer + 1)
                    if j == 0 and unit == 1:
                        need(pe, mT_taken, 2 * m + 2)
                        need(pe, qkv_taken, 4 * g)
                    col = GW * ((g - GROUPS * layer) // 2) if isinstance(g, int) else (c + 2) // 2 * GW + (m - c - GROUPS * layer) * (GW // 2)
                    t = 4 * s0 + 2 * unit + j
                    for k in range(CH):
                        mm = product(PS[:, BANK_T[2 * unit], j * GW:(j + 1) * GW],
                                     [w[:, k, t * P:(t + 1) * P] for w in XT],
                                     [w[:, k, ds(col, GW)] for w in WQKV], start=(k == 0), stop=(k == CH - 1))
                    if j == 1:
                        mm.then_inc(qkv_ready, 1)

                def turn(stack, p, bank, ready):
                    for t in range(TPB):
                        mm = pe.transpose(PS[:, bank, t * P:(t + 1) * P].bitcast(F32R),
                                          stack[:, t * HPG + 2 * p:t * HPG + 2 * p + 2, :].rearrange("p h w -> p (h w)"),
                                          ident_r[:, :])
                    mm.then_inc(ready, 1)

                def scores(u):
                    g, h, qt = m + 1, u // TPB, u % TPB
                    keys = P * (qt + 1) if layer else SEQ
                    if u in (0, 8):
                        pe.wait_ge(qT_taken, 2 * g + u // 8 + 1)
                    if u % TPB == 0:
                        pe.wait_ge(kT_taken, 4 * g + h + 1)
                    need(pe, s1_reduced, 16 * g + u - 1)
                    bank = BANK_S1[u % 2]
                    mm = pe.matmul(PS[:, bank, 0:keys], QT[s1][:, h // 2, qt * P:(qt + 1) * P],
                                   KT[s1][:, h, 0:keys], start=True, stop=(layer == 0))
                    if layer:
                        mm = pe.matmul(PS[:, bank, keys - P:keys], ident_r[:, :], mask_r[:, :],
                                       start=False, stop=True)
                    mm.then_inc(s1_ready, 1)

                def scores_t(u):
                    kt, h = u // HPG, u % HPG
                    q0 = P * kt if layer else 0
                    if u in (0, 2):
                        pe.wait_ge(mT_taken, 2 * m + 1 + u // 2)
                    need(pe, exp_done, 16 * m + u - 1)
                    bank = BANK_S2[u % 2]
                    mm = pe.matmul(PS[:, bank, q0:SEQ], KT[s0][:, h, kt * P:(kt + 1) * P],
                                   QT[s0][:, h // 2, q0:SEQ], start=True, stop=True)
                    mm.then_inc(s2_ready, 1)

                def values(m, s0, kt):
                    q0 = P * kt if layer else 0
                    pe.wait_ge(exp_done, 16 * m + 4 * kt + 4)
                    if layer:
                        pe.wait_ge(probs_masked, 4 * (m - GROUPS) + kt + 1)
                    if kt == 0:
                        need(pe, o_taken, m)
                        pe.wait_ge(v_stacked, m + 1)
                    for h in range(HPG):
                        mm = pe.matmul(PS[32 * h:32 * h + 32, BANK_O, q0:SEQ], VS[s0][:, kt, h, :],
                                       PT[:, (4 * kt + h) % NRING, q0:SEQ], start=(kt == 0),
                                       stop=(kt == TPB - 1), skip_group_check=True)
                    mm.then_inc(pv_done, 1)

                for u in range(4 * TPB):
                    if has_c:
                        scores_t(u)
                    if has_c and u == 1:
                        pe.wait_ge(m_lo, 2 * m + 2)
                        pe.wait_ge(mT_taken, 2 * m + 1)
                        turn(QS[s0], 1, BANK_T[2], mT_ready)
                    if has_b:
                        scores(u)
                    if has_a and u in (0, 1):
                        project(0, u)
                    if has_o and u == 2:
                        values(m - 1, s1, TPB - 1)
                    if has_b and u == 2:
                        need(pe, ident_r_ready, 1)
                        pe.wait_ge(kT_taken, 4 * m + 6)
                        turn(QS[s1], 1, BANK_T[1], qT_ready)
                    if has_a and u in (3, 4):
                        project(1, u - 3)
                    if has_b and u == 5:
                        if has_a:
                            pe.wait_ge(qkv_taken, 4 * m + 10)
                        turn(KS[s1], 1, BANK_T[0], kT_ready)
                    if has_o and u == 5:
                        pe.wait_ge(o_taken, m)
                        if has_b:
                            pe.wait_ge(qT_taken, 2 * m + 4)
                        turn_output(BANK_T[1])
                    if has_a and u == F67[layer]:
                        pe.wait_ge(stack_lo, 3 * m + 9)
                        if has_b:
                            pe.wait_ge(kT_taken, 4 * m + 8)
                        turn(QS[s0], 0, BANK_T[0], qT_ready)
                        need(pe, ctx_done, m)
                        turn(KS[s0], 0, BANK_T[1], kT_ready)
                    if has_c and u in VALUES_AT[layer]:
                        values(m, s0, VALUES_AT[layer].index(u))
                    if c == -2 and u == 4:
                        norm_to_features(2 * layer, 1)
                    if c == GROUPS - 1 and u in (2, 3, 12):
                        context_to_features(layer, (2, 3, 12).index(u))
                    if has_b and u == 11:
                        pe.wait_ge(m_lo, 2 * m + 3)
                        if has_a:
                            pe.wait_ge(qkv_taken, 4 * m + 12)
                        turn(QS[s1], 0, BANK_T[2], mT_ready)
                if c == GROUPS - 1:
                    values(m, s0, TPB - 1)

            def turn_output(bank):
                for t in range(TPB):
                    mm = pe.transpose(PS[:, bank, t * P:(t + 1) * P], OS[:, t * P:(t + 1) * P], ident[:, :])
                mm.then_inc(oT_ready, 1)

            def attention(layer):
                base = GROUPS * layer
                for c in range(-2, GROUPS):
                    attention_step(layer, base + c, c)
                project_out(layer, 0)
                pe.wait_ge(o_taken, base + GROUPS)
                turn_output(BANK_T[2])
                for t in range(1, TPB):
                    project_out(layer, t)
                context_to_features(layer, 3)
                for t in range(TPB, TILES):
                    project_out(layer, t)

            def gate_up(i, c, half):
                e = 4 * i + c
                k = 2 * e + half
                if half == 0:
                    pe.wait_ge(we_lo, e + 1)
                need(pe, h_done, k - 1 if not isinstance(k, int) or k >= 2 else 0)
                W = WE[c % 4]
                for bank, w0 in ((BANK_G[half], 0), (BANK_U[half], CH * P)):
                    for j in range(CH):
                        mm = product(PS[:, bank, :], [w[:, w0 + j * P:w0 + (j + 1) * P] for w in W],
                                     [w[:, j, half * SEQ:(half + 1) * SEQ] for w in XT],
                                     start=(j == 0), stop=(j == CH - 1))
                mm.then_inc(gu_ready, 1)

            def down_sum(c, half):
                k = 2 * c + half
                pe.wait_ge(h_lo, k + 1)
                W, H = WE[c % 4], HR[k % 4]
                for t in range(TPB):
                    tile = TPB * half + t
                    mm = product(PS[:, BANK_Y[tile // 2], tile % 2 * DM:(tile % 2 + 1) * DM],
                                 [w[:, t * P:(t + 1) * P] for w in H], [w[:, 2 * CH * P:] for w in W],
                                 start=(c == STREAM - FFN_CHUNKS and t % 2 == 0), stop=(c == STREAM - 1), skip=True)
                    if c == STREAM - 1 or t == TPB - 1:
                        mm.then_inc(y_ready, 1 if c == STREAM - 1 else 4)

            def down(i, c, half):
                k = 8 * i + 2 * c + half
                pe.wait_ge(h_lo, k + 1)
                W, H = WE[c % 4], HR[(2 * c + half) % 4]
                for t in range(TPB):
                    need(pe, y_added, 4 * k + t - 3 if not isinstance(k, int) or k else 0)
                    product(PS[:, BANK_Y[t], 0:DM], [w[:, t * P:(t + 1) * P] for w in H],
                            [w[:, 2 * CH * P:] for w in W]).then_inc(y_ready, 1)

            def router_logits(half):
                features_there(10 + 2 * half)
                cols = slice(half * SEQ, (half + 1) * SEQ)
                for c in range(CH):
                    mm = product(PS[0:EXPERTS, BANK_LT[half], :], [w[:, c, :] for w in GWT],
                                 [w[:, c, cols] for w in XT], start=(c == 0), stop=(c == CH - 1))
                mm.then_inc(lT_ready, 1)

            def turn_logits():
                pe.wait_ge(lT_taken, 2)
                for t in range(TILES):
                    mm = pe.transpose(PS[:, BANK_LOGITS, t * EXPERTS:(t + 1) * EXPERTS],
                                      LT[:, t // TPB, t % TPB * P:(t % TPB + 1) * P],
                                      ident[0:EXPERTS, 0:EXPERTS])
                mm.then_inc(logits_ready, 1)

            def units(pairs):
                for i, c in pairs:
                    for half in range(2):
                        gate_up(i, c, half)
                        down(i, c - 1, half)

            pe.wait_ge(ident_loaded, 16)
            for layer in range(2):
                norm_to_features(2 * layer, 0)
                attention(layer)
                for half in range(2):
                    norm_to_features(2 * layer + 1, half)
                if layer == 0:
                    pe.wait_ge(consts_ready, 3)
                    router_logits(0)
                    gate_up(0, 0, 0)
                    router_logits(1)
                    turn_logits()
                    gate_up(0, 0, 1)
                    pe.wait_ge(router_exp, 1)
                    units([(0, 1)])
                    with pe.Fori(0, 3) as i:
                        units((i, c) for c in range(2, 6))
                    units((0, c) for c in range(14, 1 + EXPERTS))
                    for half in range(2):
                        down(0, EXPERTS, half)
                else:
                    for half in range(2):
                        features_there(22 + 2 * half)
                        gate_up(0, 17, half)
                    for c in range(18, STREAM):
                        for half in range(2):
                            gate_up(0, c, half)
                            down_sum(c - 1, half)
                    for half in range(2):
                        down_sum(STREAM - 1, half)

        @block.vector
        def _(dve):
            own = Steps(dve_self)

            def after_own():
                dve.wait_ge(dve_self, own.n)

            def statistics(t):
                own.done(dve.bn_stats(STATS[:, t, :], X[:, t, :]))

            def variances(half):
                after_own()
                tiles = slice(TPB * half, TPB * (half + 1))
                for t in range(TPB * half, TPB * (half + 1)):
                    own.done(dve.bn_aggr(MV[:, t, :], STATS[:, t, :]))
                after_own()
                dve.tensor_scalar(VE[:, tiles], MV[:, tiles, 1], EPS, None, ALU.add).then_inc(var_ready, 1)

            def normalise(l, half):
                tiles = slice(TPB * half, TPB * (half + 1))
                dve.wait_ge(std_ready, 2 * l + half + 1)
                own.done(dve.reciprocal(RSTD[:, tiles], SD[:, tiles]))
                after_own()
                for t in range(TPB * half, TPB * (half + 1)):
                    ins = dve.tensor_scalar(XN[:, t, :], X[:, t, :], MV[:, t, 0:1], RSTD[:, t:t + 1],
                                            ALU.subtract, ALU.mult)
                ins.then_inc(normed, 1)

            def take_lo(n, fill, bank):
                half, c = fill
                cols = slice(half * SEQ, (half + 1) * SEQ)
                dve.wait_ge(xT_hi_done, n + 1)
                dve.tensor_tensor(XT[1][:, c, cols], PS[:, bank, :], XT[0][:, c, cols].bitcast(F32),
                                  ALU.subtract).then_inc(xT_lo_done, 1)

            def norm_lo(l, half):
                n = (0, 8, 12, 20)[l] + 2 * half
                for c in range(CH):
                    take_lo(n + c, (half, c), BANK_NORM[2 * half + c])

            def context_both(layer, f):
                half, c = CTX_FILLS[f]
                n = 12 * layer + 4 + f
                dve.wait_ge(xT_ready, n + 1)
                dve.tensor_copy(XT[0][:, c, half * SEQ:(half + 1) * SEQ],
                                PS[:, BANK_CTX[f], :]).then_inc(xT_hi_done, 1)
                take_lo(n, (half, c), BANK_CTX[f])

            def split_weights(n):
                dst, src = ((WQKV, stage_qkv), (WO, stage_wo))[n]
                dve.wait_ge(wsplit_hi, n + 1)
                dve.tensor_tensor(dst[1][:, :, :], src[:, :, :], dst[0][:, :, :].bitcast(F32),
                                  ALU.subtract).then_inc(wsplit_lo, 1)

            def attention_step(layer, m, c):
                s0, s1 = c % 2, (c + 1) % 2
                has_c, has_b, has_a, has_o = (in_layer(c, d) for d in (0, 1, 2, -1))

                def take_qkv(unit):
                    g = m + 2
                    dve.wait_ge(qkv_ready, 2 * g + unit + 1)
                    if unit == 0:
                        need(dve, stack_lo, 3 * g - 3)
                        need(dve, stack_hi, 2 * g - 2)
                        need(dve, v_stacked, g - 1)
                        if layer == 0:
                            need(dve, rope_part, 6 * g - 6)
                    if c == -2 and unit == 0:
                        dve.wait_ge(rows_in, 32 * (layer + 1))
                        dve.wait_ge(zeroed, 1)
                    col = GW * ((g - GROUPS * layer) // 2) if isinstance(g, int) else (c + 2) // 2 * GW + (m - c - GROUPS * layer) * (GW // 2)
                    got = PS[:, BANK_T[2 * unit], 0:2 * GW].rearrange("p (t w) -> p t w", t=2)
                    rows = slice(2 * HPG * unit, 2 * HPG * (unit + 1))
                    bias = BQKV[:, ds(col, GW)].rearrange("p (a w) -> p a w", a=3).unsqueeze(2)
                    dve.tensor_tensor(QKV[s0][:, :, rows, :].rearrange("p a (t h) d -> p a t (h d)", t=2),
                                      got.rearrange("p t (a w) -> p a t w", a=3),
                                      bias.broadcast_to([P, 3, 2, HPG * HD]), ALU.add).then_inc(qkv_taken, 2)

                def rope(unit):
                    rows = slice(2 * HPG * unit, 2 * HPG * (unit + 1))
                    if unit == 0:
                        dve.wait_ge(rope_in, 16)
                    dve.wait_ge(qkv_taken, 2 * unit + 2)
                    need(dve, rope_done, unit)
                    dve.tensor_tensor(*rope_cos(s0, rows)).then_inc(rope_part, 1)
                    for j in range(2):
                        dve.tensor_tensor(*rope_sin(s0, rows, j)).then_inc(rope_part, 1)
                    dve.wait_ge(rope_part, 3 * unit + 3)
                    dve.tensor_tensor(*rope_sum(s0, rows)).then_inc(rope_done, 1)

                def split_lo():
                    g = m + 2
                    dve.wait_ge(stack_hi, 2 * g + 2)
                    dve.memset(QS[s0][:, :, 3 * HD:3 * HD + 2].bitcast(F32), 0.0).then_inc(stack_lo, 1)
                    dve.tensor_tensor(*q_lo(layer, s0)).then_inc(stack_lo, 1)
                    dve.tensor_tensor(*k_lo(layer, s0)).then_inc(stack_lo, 1)

                def take_qT(g, s, p):
                    dve.wait_ge(qT_ready, 2 * g + p + 1)
                    if p == 0:
                        need(dve, s2_ready, 16 * g - 18)
                    dve.tensor_copy(QT[s][:, p, :], PS[:, BANK_T[p], :]).then_inc(qT_taken, 1)

                def reduce(u):
                    g, h, qt = m + 1, u // TPB, u % TPB
                    keys = P * (qt + 1) if layer else SEQ
                    dve.wait_ge(s1_ready, 16 * g + u + 1)
                    dve.tensor_reduce(MX[s1][:, h, qt:qt + 1], PS[:, BANK_S1[u % 2], 0:keys], AX.X,
                                      ALU.max).then_inc(s1_reduced, 1)

                def split_max(p):
                    g = m + 1
                    dve.wait_ge(s1_reduced, 16 * g + 8 * p + 8)
                    stack = QS[s1][:, :, :].rearrange("p (t h) w -> p t h w", t=TPB)
                    mx = MX[s1][:, 2 * p:2 * p + 2, :].rearrange("p h t -> p t h")
                    hi = stack[:, :, 2 * p:2 * p + 2, 3 * HD]
                    lo = stack[:, :, 2 * p:2 * p + 2, 3 * HD + 1]
                    dve.tensor_scalar(hi, mx, -1.0, None, ALU.mult).then_inc(m_hi, 1)
                    dve.wait_ge(m_hi, 2 * g + p + 1)
                    dve.scalar_tensor_tensor(lo, mx, -1.0, hi.bitcast(F32), ALU.mult,
                                             ALU.subtract).then_inc(m_lo, 1)

                for u in range(4 * TPB):
                    if has_b:
                        reduce(u)
                    if has_a and u in (1, 5):
                        take_qkv(u // 4)
                    if c == -2 and u == 6:
                        if layer == 0:
                            for unit in range(2):
                                rope(unit)
                        split_lo()
                        norm_lo(2 * layer, 1)
                        if layer == 0:
                            split_weights(1)
                    if c == GROUPS - 1 and u in (2, 3, 12):
                        context_both(layer, (2, 3, 12).index(u))
                    if has_b and u == 3:
                        take_qT(m + 1, s1, 1)
                    if has_b and u == 8:
                        split_max(0)
                    if has_o and u == 9:
                        normalise_context(layer, m - 1, c - 1, BANK_T[1])
                    if has_a and u == F67[layer]:
                        take_qT(m + 2, s0, 0)
                if has_b:
                    split_max(1)

            def normalise_context(layer, m, c, bank):
                T = PS[:, bank, :].rearrange("p (r w) -> p r w", w=32)
                dve.wait_ge(oT_ready, m + 1)
                dve.reciprocal(RD[:, :], T[:, :, HD]).then_inc(rd_done, 1)
                dve.wait_ge(rd_done, m + 1)
                t0 = TPB * (c % 2)
                col = HPG * HD * (c // 2) if isinstance(m, int) else (m - c - GROUPS * layer) * (HPG * HD // 2) + c // 2 * HPG * HD
                dst = XN[:, t0:t0 + TPB, ds(col, HPG * HD)].rearrange("p t (h d) -> p t h d", h=HPG)
                src = T[:, :, 0:HD].rearrange("p (t h) d -> p t h d", t=TPB)
                rd = RD[:, :].rearrange("p (t h) -> p t h", t=TPB).unsqueeze(3).broadcast_to([P, TPB, HPG, HD])
                dve.tensor_tensor(dst, src, rd, ALU.mult).then_inc(ctx_done, 1)

            def attention(layer):
                base = GROUPS * layer
                for c in range(-2, GROUPS):
                    attention_step(layer, base + c, c)
                residual(layer, 0)
                normalise_context(layer, base + GROUPS - 1, GROUPS - 1, BANK_T[2])
                residual(layer, 1)
                residual(layer, 2)
                take_lo(12 * layer + 7, CTX_FILLS[3], BANK_CTX[3])
                residual(layer, 3)
                statistics_of(layer, range(TPB))
                variances(0)
                residual(layer, 4)
                residual(layer, 5)
                normalise(2 * layer + 1, 0)
                residual(layer, 6)
                residual(layer, 7)
                norm_lo(2 * layer + 1, 0)
                statistics_of(layer, range(TPB, TILES))
                variances(1)
                normalise(2 * layer + 1, 1)
                norm_lo(2 * layer + 1, 1)

            def residual(layer, t):
                dve.wait_ge(proj_out_ready, TILES * layer + t + 1)
                if t == 0:
                    dve.wait_ge(bias_added, layer + 1)
                dve.tensor_tensor(X[:, t, :], PS[:, BANK_PROJ[t % 4], 0:DM], X[:, t, :],
                                  ALU.add).then_inc(resid_done, 1)

            def statistics_of(layer, tiles):
                dve.wait_ge(resid_done, TILES * layer + tiles[-1] + 1)
                for t in tiles:
                    statistics(t)

            def step(ins):
                own.done(ins)
                after_own()

            sc = R["e"]

            def router_groups():
                dve.wait_ge(tables_in, 16 * 7)
                own.done(dve.tensor_copy(TIEB[:, :, :], TIES[:, :, :]))
                dve.wait_ge(router_exp, 1)
                step(dve.tensor_scalar(R["s"][:, :, :], R["e"][:, :, :], 1.0, None, ALU.add))
                step(dve.reciprocal(R["e"][:, :, :], R["s"][:, :, :]))
                step(dve.tensor_tensor(R["b"][:, :, :], sc[:, :, :],
                                       EB[:, :].unsqueeze(1).broadcast_to([P, TILES, EXPERTS]), ALU.add))
                b4 = R["b"][:, :, :].rearrange("p t (g a c) -> p (t g) a c", g=NGRP, a=2)
                fl = {n: v[:, :, :, :].rearrange("p t g w -> p (t g) w") for n, v in RG.items()}
                own.done(dve.tensor_tensor(fl["hi"][:, :, :], b4[:, :, :, 0], b4[:, :, :, 1], ALU.max))
                step(dve.tensor_tensor(fl["lo"][:, :, :], b4[:, :, :, 0], b4[:, :, :, 1], ALU.min))
                own.done(dve.tensor_tensor(fl["t1"][:, :, :], fl["hi"][:, :, 0:1], fl["hi"][:, :, 1:2], ALU.max))
                own.done(dve.tensor_tensor(fl["a"][:, :, :], fl["hi"][:, :, 0:1], fl["hi"][:, :, 1:2], ALU.min))
                step(dve.tensor_tensor(fl["b"][:, :, :], fl["lo"][:, :, 0:1], fl["lo"][:, :, 1:2], ALU.max))
                step(dve.tensor_tensor(fl["a"][:, :, :], fl["a"][:, :, :], fl["b"][:, :, :], ALU.max))
                step(dve.tensor_tensor(fl["s"][:, :, :], fl["t1"][:, :, :], fl["a"][:, :, :], ALU.add))
                gs = RG["s"][:, :, :, 0]
                gmine = gs.unsqueeze(3).broadcast_to([P, TILES, NGRP, NGRP])
                gother = gs.unsqueeze(2).broadcast_to([P, TILES, NGRP, NGRP])
                own.done(dve.tensor_tensor(CG[:, 0], gother, gmine, ALU.is_gt))
                step(dve.tensor_tensor(CG[:, 1], gother, gmine, ALU.is_equal))
                tg = TIEG[:, :, :].unsqueeze(1).broadcast_to([P, TILES, NGRP, NGRP])
                step(dve.tensor_tensor(CG[:, 1], CG[:, 1], tg, ALU.mult))
                step(dve.tensor_tensor(CG[:, 0], CG[:, 0], CG[:, 1], ALU.add))
                step(dve.tensor_reduce(RKG[:, :, :], CG[:, 0], AX.X, ALU.add))
                step(dve.tensor_scalar(RKG[:, :, :], RKG[:, :, :], float(2), None, ALU.is_lt))
                rk = RKG[:, :, :].unsqueeze(3).broadcast_to([P, TILES, NGRP, GSZ])
                v4 = R["v"][:, :, :].rearrange("p t (g c) -> p t g c", g=NGRP)
                b44 = R["b"][:, :, :].rearrange("p t (g c) -> p t g c", g=NGRP)
                g4 = R["gm"][:, :, :].rearrange("p t (g c) -> p t g c", g=NGRP)
                own.done(dve.tensor_scalar(g4, rk, 1.0, -NEG, ALU.subtract, ALU.mult))
                step(dve.tensor_tensor(v4, b44, rk, ALU.mult))
                step(dve.tensor_tensor(R["v"][:, :, :], R["v"][:, :, :], R["gm"][:, :, :], ALU.add))

            mine_other = [P, TILES, EXPERTS, EXPERTS]
            mine = R["v"][:, :, :].unsqueeze(3).broadcast_to(mine_other)
            other = R["v"][:, :, :].unsqueeze(2).broadcast_to(mine_other)
            better, equal = (w.rearrange("p (t e) c -> p t e c", e=EXPERTS) for w in CMP)

            def router_better():
                step(dve.tensor_tensor(better, other, mine, ALU.is_gt))

            def router_equal():
                step(dve.tensor_tensor(equal, other, mine, ALU.is_equal))

            def router_weights():
                step(dve.tensor_tensor(equal, equal, TIEB[:, :, :].unsqueeze(1).broadcast_to(mine_other), ALU.mult))
                step(dve.tensor_tensor(better, better, equal, ALU.add))
                step(dve.tensor_reduce(RK[:, :, :], better, AX.X, ALU.add))
                step(dve.tensor_scalar(RK[:, :, :], RK[:, :, :], float(TOPK), None, ALU.is_lt))
                step(dve.tensor_tensor(R["w"][:, :, :], RK[:, :, :], sc[:, :, :], ALU.mult))
                step(dve.tensor_reduce(WSUM[:, :], R["w"][:, :, :], AX.X, ALU.add))
                step(dve.tensor_scalar(WSUM[:, :], WSUM[:, :], 1e-20, None, ALU.add))
                step(dve.reciprocal(WREC[:, :], WSUM[:, :]))
                step(dve.tensor_tensor(R["c"][:, :, :], R["w"][:, :, :],
                                       WREC[:, :].unsqueeze(2).broadcast_to([P, TILES, EXPERTS]), ALU.mult))
                dve.tensor_scalar(R["c"][:, :, :], R["c"][:, :, :], 2.5, None, ALU.mult).then_inc(routed, 1)
                dve.wait_ge(routed, 1)

            def hidden(i, c, half, ffn=None):
                k = 8 * i + 2 * c + half
                dve.wait_ge(silu_done, k + 1)
                need(dve, h_lo, k - 1 if not isinstance(k, int) or k >= 2 else 0)
                if ffn is None:
                    ins = dve.tensor_tensor(HF[half], PS[:, BANK_U[half], :], SG[half], ALU.mult)
                else:
                    ins = dve.scalar_tensor_tensor(HF[half], PS[:, BANK_U[half], :], SSC[:, ffn, 1:2],
                                                   SG[half], ALU.mult, ALU.mult)
                ins.then_inc(h_done, 1)

            def add_down(i, c, half):
                k = 8 * i + 2 * c + half
                for t in range(TPB):
                    dve.wait_ge(y_ready, 4 * k + t + 1)
                    tile = half * TPB + t
                    y = PS[:, BANK_Y[t], 0:DM]
                    need(dve, y_added, 4 * k + t - 7 if not isinstance(k, int) or 4 * k + t >= 8 else 0)
                    if isinstance(i, int) and i == 0 and c == 0:
                        ins = dve.tensor_tensor(X[:, tile, :], y, X[:, tile, :], ALU.add)
                    else:
                        w = R["c"][:, tile, ds(4 * i + c - 1, 1)]
                        ins = dve.scalar_tensor_tensor(X[:, tile, :], y, w, X[:, tile, :],
                                                       ALU.mult, ALU.add)
                    ins.then_inc(y_added, 1)

            def finish(half):
                k = 2 * (STREAM - 1) + half
                for t in range(TPB):
                    tile = half * TPB + t
                    dve.wait_ge(y_ready, 4 * k + t // 2 * 2 + 2)
                    y = PS[:, BANK_Y[tile // 2], tile % 2 * DM:(tile % 2 + 1) * DM]
                    dve.tensor_tensor(XN[:, tile, :], y, DSC[:, :], ALU.mult).then_inc(out_scaled, 1)
                    if t:
                        dve.wait_ge(out_scaled, tile)
                        dve.tensor_tensor(X[:, tile - 1, :], X[:, tile - 1, :], XN[:, tile - 1, :],
                                          ALU.add).then_inc(out_ready, 1)
                dve.wait_ge(out_scaled, tile + 1)
                dve.tensor_tensor(X[:, tile, :], X[:, tile, :], XN[:, tile, :],
                                  ALU.add).then_inc(out_ready, 1)

            for half in range(2):
                dve.wait_ge(x_in[half], 16)
                for t in range(TPB * half, TPB * (half + 1)):
                    statistics(t)
                variances(half)
            normalise(0, 0)
            split_weights(0)
            norm_lo(0, 0)
            normalise(0, 1)
            attention(0)
            router_groups()
            hidden(0, 0, 0)
            hidden(0, 0, 1)
            router_better()
            hidden(0, 1, 0)
            add_down(0, 0, 0)
            router_equal()
            hidden(0, 1, 1)
            add_down(0, 0, 1)
            hidden(0, 2, 0)
            router_weights()
            add_down(0, 1, 0)
            hidden(0, 2, 1)
            add_down(0, 1, 1)
            for c in range(3, 1 + EXPERTS):
                for half in range(2):
                    hidden(0, c, half)
                    add_down(0, c - 1, half)
            for half in range(2):
                add_down(0, EXPERTS, half)
                dve.wait_ge(y_added, 8 * EXPERTS + 4 * half + 4)
                for t in range(TPB * half, TPB * (half + 1)):
                    statistics(t)
                variances(half)
            normalise(2, 0)
            norm_lo(2, 0)
            normalise(2, 1)
            attention(1)
            for half in range(2):
                hidden(0, 17, half, 0)
            for c in range(18, STREAM):
                for half in range(2):
                    hidden(0, c, half, c - 17)
            for half in range(2):
                finish(half)

        @block.scalar
        def _(act):
            def root(l, half):
                tiles = slice(TPB * half, TPB * (half + 1))
                act.wait_ge(var_ready, 2 * l + half + 1)
                act.activation(SD[:, tiles], VE[:, tiles], ACT.Sqrt).then_inc(std_ready, 1)

            def take_hi(n, fill, bank):
                half, c = fill
                act.wait_ge(xT_ready, n + 1)
                act.copy(XT[0][:, c, half * SEQ:(half + 1) * SEQ], PS[:, bank, :]).then_inc(xT_hi_done, 1)

            def norm_hi(l, half):
                n = (0, 8, 12, 20)[l] + 2 * half
                for c in range(CH):
                    take_hi(n + c, (half, c), BANK_NORM[2 * half + c])

            def attention_step(layer, m, c):
                s0, s1 = c % 2, (c + 1) % 2
                has_c, has_b, has_a, has_o = (in_layer(c, d) for d in (0, 1, 2, -1))

                def take_kT(g, s, h):
                    p = h // 2
                    act.wait_ge(kT_ready, 2 * g + p + 1)
                    if h == 0:
                        need(act, s2_ready, 16 * g - 18)
                        need(act, zeroed, 1)
                    if h == 2:
                        need(act, s2_ready, 16 * g - 16)
                    rows = slice(64 * (h % 2), 64 * (h % 2) + 64)
                    act.copy(KT[s][rows, h, :], PS[rows, BANK_T[1 - p], :]).then_inc(kT_taken, 1)

                def take_mT(g, s, p):
                    act.wait_ge(mT_ready, 2 * g + p + 1)
                    act.copy(QT[s][:, p, :], PS[:, BANK_T[2], :]).then_inc(mT_taken, 1)

                def split_hi(part):
                    g = m + 2
                    src = QK[s0] if layer else ROPED[s0]
                    if part == 0:
                        act.wait_ge(qkv_taken if layer else rope_done, 4 * g + 4 if layer else 2 * g + 2)
                    need(act, mT_ready, 2 * g - 2)
                    need(act, kT_ready, 2 * g - 2)
                    if c == -2:
                        act.wait_ge(zeroed, 1)
                    n = TPB * HPG
                    if part == 0:
                        q2 = QS[s0][:, :, 0:2 * HD].rearrange("p r (a d) -> p r a d", a=2)
                        act.copy(q2, src[:, 0].unsqueeze(2).broadcast_to([P, n, 2, HD])).then_inc(stack_hi, 1)
                        return
                    k2 = KS[s0][:, :, :].rearrange("p r (a b d) -> p r a b d", a=2, b=2)[:, :, :, 0, :]
                    act.copy(k2, src[:, 1].unsqueeze(2).broadcast_to([P, n, 2, HD])).then_inc(stack_hi, 1)

                def exponentials(u):
                    kt = u // HPG
                    q0 = P * kt if layer else 0
                    act.wait_ge(s2_ready, 16 * m + u + 1)
                    act.activation(PT[:, u % NRING, q0:SEQ], PS[:, BANK_S2[u % 2], q0:SEQ], ACT.Exp,
                                   scale=SCALE).then_inc(exp_done, 1)

                for u in range(4 * TPB):
                    if has_c:
                        exponentials(u)
                    if has_c and u == 1:
                        take_mT(m, s0, 1)
                    if has_o and u == 3:
                        take_output(m - 1)
                    if has_b and u in (5, 6):
                        take_kT(m + 1, s1, u - 3)
                    if has_a and u in (9, 10):
                        split_hi(u - 9)
                    if has_b and u == 11:
                        take_mT(m + 1, s1, 0)
                    if layer == 0 and u == 10 and c in (GROUPS - 2, GROUPS - 1):
                        split_expert(0, c - GROUPS + 2)
                    if has_a and u - F67[layer] in (0, 1):
                        take_kT(m + 2, s0, u - F67[layer])

            def take_output(m):
                act.wait_ge(pv_done, 4 * m + 4)
                need(act, oT_ready, m)
                act.copy(OS[:, :], PS[:, BANK_O, :]).then_inc(o_taken, 1)

            def attention(layer):
                for c in range(-2, GROUPS):
                    attention_step(layer, GROUPS * layer + c, c)
                take_output(GROUPS * layer + GROUPS - 1)

            def split_weights(n):
                dst, src, s = ((WQKV, stage_qkv, wqkv_in), (WO, stage_wo, wo_in))[n % 2]
                act.wait_ge(s, 16 * (n // 2 + 1))
                act.copy(dst[0][:, :, :], src[:, :, :]).then_inc(wsplit_hi, 1)

            def split_expert(i, c):
                e = 4 * i + c
                act.wait_ge(stream_in[c % 2], 32 * i + 16 * (c // 2 + 1))
                need(act, y_ready, 8 * (e - 3) if not isinstance(e, int) or e >= 4 else 0)
                act.copy(WE[c % 4][0][:, :], stage_w[c % 2][:, :]).then_inc(we_hi, 1)

            def unit(i, c, half, ffn=None):
                k = 8 * i + 2 * c + half
                act.wait_ge(gu_ready, k + 1)
                need(act, h_done, k - 1 if not isinstance(k, int) or k >= 2 else 0)
                act.activation(SG[half], PS[:, BANK_G[half], :], ACT.Silu,
                               scale=1.0 if ffn is None else SSC[:, ffn, 0:1]).then_inc(silu_done, 1)
                act.wait_ge(h_done, k + 1)
                need(act, y_ready, 4 * (k - 3) if not isinstance(k, int) or k >= 4 else 0)
                act.copy(HR[(2 * c + half) % 4][0][:, :], HF[half]).then_inc(h_hi, 1)

            act.wait_ge(ident_loaded, 16)
            act.copy(ident_r[:, :], ident[:, :]).then_inc(ident_r_ready, 1)
            for half in range(2):
                root(0, half)
            split_weights(0)
            for half in range(2):
                norm_hi(0, half)
            split_weights(1)
            act.wait_ge(tables_in, 16 * 7)
            act.copy(mask_r[:, :], mask_in[:, :]).then_inc(consts_ready, 1)
            act.copy(GWT[0][:, :, :], GWS[:, :, :]).then_inc(consts_ready, 1)
            for layer in range(2):
                if layer:
                    for half in range(2):
                        root(2, half)
                    for half in range(2):
                        norm_hi(2, half)
                attention(layer)
                take_hi(12 * layer + 7, CTX_FILLS[3], BANK_CTX[3])
                if layer == 0:
                    split_expert(0, 2)
                for half in range(2):
                    root(2 * layer + 1, half)
                    norm_hi(2 * layer + 1, half)
                if layer == 0:
                    for half in range(2):
                        act.wait_ge(lT_ready, half + 1)
                        act.copy(LT[:, half, :], PS[0:EXPERTS, BANK_LT[half], :]).then_inc(lT_taken, 1)
                    act.wait_ge(logits_ready, 1)
                    act.activation(R["e"][:, :, :].rearrange("p t e -> p (t e)"),
                                   PS[:, BANK_LOGITS, 0:TILES * EXPERTS], ACT.Exp,
                                   scale=-1.0).then_inc(router_exp, 1)
                    for half in range(2):
                        unit(0, 0, half)
                    for c in range(1, 1 + EXPERTS):
                        for half in range(2):
                            unit(0, c, half)
                            if half == 0:
                                split_expert(0, c + 2)
                        if c >= EXPERTS - 1:
                            split_weights(c - EXPERTS + 3)
                else:
                    for c in range(17, STREAM):
                        for half in range(2):
                            unit(0, c, half, c - 17)
                            if half == 0 and c + 2 < STREAM:
                                split_expert(0, c + 2)

        @block.gpsimd
        def _(pool):
            own = Steps(pool_self)
            for s in range(2):
                own.done(pool.memset(QS[s][:, :, :].bitcast(F32), 0.0))
                own.done(pool.memset(KS[s][:, :, :].bitcast(F32), 0.0))
                own.done(pool.memset(KT[s][:, :, :].bitcast(F32), 0.0))
                own.done(pool.memset(VS[s][:, :, :, :], 0.0))
            pool.wait_ge(pool_self, own.n)
            for s in range(2):
                own.done(pool.memset(KS[s][:, :, 3 * HD:3 * HD + 2].bitcast(F32), 1.0))
                own.done(pool.memset(VS[s][:, :, :, HD:HD + 1], 1.0))
            pool.wait_ge(pool_self, own.n)
            pool.memset(RD[:, :], 0.0).then_inc(zeroed, 1)

            def split_weights(n):
                dst, src = ((WQKV, stage_qkv), (WO, stage_wo))[n % 2]
                pool.wait_ge(wsplit_hi, n + 1)
                pool.tensor_tensor(dst[1][:, :, :], src[:, :, :], dst[0][:, :, :].bitcast(F32),
                                   ALU.subtract).then_inc(wsplit_lo, 1)

            def split_expert(i, c):
                pool.wait_ge(we_hi, 4 * i + c + 1)
                pool.tensor_tensor(WE[c % 4][1][:, :], stage_w[c % 2][:, :],
                                   WE[c % 4][0][:, :].bitcast(F32), ALU.subtract).then_inc(we_lo, 1)

            def attention_step(layer, m, c):
                if in_layer(c, 1):
                    s1 = (c + 1) % 2
                    pool.wait_ge(qkv_taken, 4 * m + 8)
                    need(pool, pv_done, 4 * m)
                    pool.tensor_copy(VS[s1][:, :, :, 0:HD],
                                     QKV[s1][:, 2].rearrange("p (t h) d -> p t h d", h=HPG)).then_inc(v_stacked, 1)
                if layer and in_layer(c, 0):
                    mask_probs(m, 0)
                    mask_probs(m, 1)
                if in_layer(c, 2) and c > -2:
                    rope_and_split(layer, m, c)
                if layer and in_layer(c, 0):
                    mask_probs(m, 2)
                    mask_probs(m, 3)

            def mask_probs(m, kt):
                pool.wait_ge(exp_done, 16 * m + 4 * kt + 4)
                own = PT[:, 4 * kt % NRING:4 * kt % NRING + HPG, P * kt:P * (kt + 1)]
                pool.affine_select(out=own, in_=own, compare_op=ALU.is_ge, fill=0.0, base=0,
                                   pattern=[[0, HPG], [1, P]], channel_multiplier=-1).then_inc(probs_masked, 1)

            def rope_and_split(layer, m, c):
                g, s0 = m + 2, c % 2
                if layer == 0:
                    for unit in range(2):
                        rows = slice(2 * HPG * unit, 2 * HPG * (unit + 1))
                        pool.wait_ge(qkv_taken, 4 * g + 2 * unit + 2)
                        pool.wait_ge(rope_done, 2 * g + unit)
                        need(pool, stack_hi, 2 * g - 2)
                        pool.tensor_tensor(*rope_cos(s0, rows)).then_inc(rope_part, 1)
                        for j in range(2):
                            pool.tensor_tensor(*rope_sin(s0, rows, j)).then_inc(rope_part, 1)
                        pool.wait_ge(rope_part, 6 * g + 3 * unit + 3)
                        pool.tensor_tensor(*rope_sum(s0, rows)).then_inc(rope_done, 1)
                pool.wait_ge(stack_hi, 2 * g + 2)
                pool.memset(QS[s0][:, :, 3 * HD:3 * HD + 2].bitcast(F32), 0.0).then_inc(stack_lo, 1)
                pool.tensor_tensor(*q_lo(layer, s0)).then_inc(stack_lo, 1)
                pool.tensor_tensor(*k_lo(layer, s0)).then_inc(stack_lo, 1)

            def attention(layer):
                for c in range(-2, GROUPS):
                    attention_step(layer, GROUPS * layer + c, c)
                    if c == -2 and layer == 0:
                        pool.wait_ge(consts_ready, 2)
                        pool.tensor_tensor(GWT[1][:, :, :], GWS[:, :, :], GWT[0][:, :, :].bitcast(F32),
                                           ALU.subtract).then_inc(consts_ready, 1)
                    if c == GROUPS - 2:
                        add_bias(layer)
                    if c >= GROUPS - 2 and layer == 0:
                        split_expert(0, c - GROUPS + 2)

            def unit(i, c, half):
                k = 8 * i + 2 * c + half
                pool.wait_ge(h_hi, k + 1)
                H = HR[(2 * c + half) % 4]
                pool.tensor_tensor(H[1][:, :], HF[half], H[0][:, :].bitcast(F32),
                                   ALU.subtract).then_inc(h_lo, 1)

            def add_bias(layer):
                pool.wait_ge(rows_in, 32 * (layer + 1))
                pool.wait_ge(normed, 4 * layer + 2)
                pool.tensor_tensor(X[:, :, :], X[:, :, :],
                                   BO[:, :].unsqueeze(1).broadcast_to([P, TILES, DM]),
                                   ALU.add).then_inc(bias_added, 1)

            pool.wait_ge(rope_in, 16)
            attention(0)
            split_expert(0, 2)
            for half in range(2):
                unit(0, 0, half)
            for c in range(1, 1 + EXPERTS):
                for half in range(2):
                    unit(0, c, half)
                    if half == 0:
                        split_expert(0, c + 2)
                if c >= EXPERTS - 1:
                    split_weights(c - EXPERTS + 3)
            attention(1)
            for c in range(17, STREAM):
                for half in range(2):
                    unit(0, c, half)
                    if half == 0 and c + 2 < STREAM:
                        split_expert(0, c + 2)


def _chunks(w):
    return np.ascontiguousarray(w.reshape(-1, P, w.shape[1]).transpose(1, 0, 2))


def _by_group(w):
    lead = w.shape[:-1]
    w = w.reshape(*lead, 3, HEADS // HPG, HPG * HD)
    return np.ascontiguousarray(np.swapaxes(w, -3, -2)).reshape(*lead, 3 * DM)


def _stream(gate, up, down):
    g, u = (_chunks(w.T).reshape(P, CH * P) for w in (gate, up))
    return np.concatenate([g, u, down.T], axis=1)


def _rope_tables():
    inv = 1.0 / 10000.0 ** (np.arange(0, HD, 2, dtype=np.float32) / HD)
    freqs = np.outer(np.arange(SEQ, dtype=np.float32), inv)
    emb = np.concatenate([freqs, freqs], axis=-1)
    cos, sin = np.cos(emb).astype(np.float32), np.sin(emb).astype(np.float32)
    sin[:, :HD // 2] = -sin[:, :HD // 2]
    both = np.stack([cos, sin]).reshape(2, TPB, P, 1, HD)
    both = np.broadcast_to(both, (2, TPB, P, HPG, HD)).transpose(2, 0, 1, 3, 4)
    return np.ascontiguousarray(both).reshape(P, 2, TPB * HPG, HD)


def kernel(**inputs):
    import concourse.bacc as _bacc
    from concourse.bass_utils import run_bass_kernel_spmd as _run

    a = {k: np.asarray(v) for k, v in inputs.items()}
    tri = np.triu(np.ones((P, P), np.float32), 1) * np.float32(NEG)
    lower = [(np.arange(n)[None, :] < np.arange(n)[:, None]).astype(np.float32).ravel() for n in (EXPERTS, NGRP)]
    pad = FFN_CHUNKS * P - FFN_INTER
    gw, uw, dw = a["L1_ffn_gate_w"], a["L1_ffn_up_w"], a["L1_ffn_down_w"]
    gw, uw = (np.concatenate([w, np.zeros((pad, DM), np.float32)]) for w in (gw, uw))
    dw = np.concatenate([dw, np.zeros((DM, pad), np.float32)], axis=1)
    rows = [slice(c * P, (c + 1) * P) for c in range(FFN_CHUNKS)]
    stream = [_stream(a["L0_ffn_shared_gate"], a["L0_ffn_shared_up"], a["L0_ffn_shared_down"])]
    stream += [_stream(a["L0_ffn_gate_proj"][e], a["L0_ffn_up_proj"][e], a["L0_ffn_down_proj"][e]) for e in range(EXPERTS)]
    stream += [_stream(gw[r], uw[r], dw[:, r]) for r in rows]
    scales = [np.concatenate([a[n], np.zeros(pad, np.float32)]).reshape(FFN_CHUNKS, P).T for n in ("L1_ffn_gate_s", "L1_ffn_up_s")]
    w0 = np.concatenate([a["L0_attn_Wq"].T, a["L0_attn_Wk"].T, a["L0_attn_Wv"].T], axis=1)
    b0 = np.concatenate([a["L0_attn_bq"], a["L0_attn_bk"], a["L0_attn_bv"]])
    arrays = {
        "x": _chunks(a["L0_attn_x"].reshape(-1, DM)),
        "wqkv": np.stack([_chunks(_by_group(w0)), _chunks(_by_group(a["L1_attn_w_qkv"]))]),
        "bqkv": np.stack([_by_group(b0), _by_group(a["L1_attn_b_qkv"])]),
        "wo": np.stack([_chunks(a["L0_attn_Wo"].T), _chunks(a["L1_attn_w_proj"])]),
        "bo": np.stack([a["L0_attn_bo"], a["L1_attn_b_proj"]]),
        "rope": _rope_tables(),
        "mask": tri,
        "ident": np.eye(P, dtype=np.float32),
        "router_w": _chunks(a["L0_ffn_gate_weight"].T),
        "router_b": a["L0_ffn_expert_bias"],
        "ties": np.concatenate(lower)[None],
        "stream_w": np.stack(stream),
        "stream_scale": np.ascontiguousarray(np.stack(scales, axis=2)),
        "down_scale": a["L1_ffn_down_s"],
    }
    nc = _bacc.Bacc("TRN2", target_bir_lowering=False, num_devices=1)
    args = [nc.dram_tensor(f"in_{n}", v.shape, F32, kind="ExternalInput").ap() for n, v in arrays.items()]
    args.append(nc.dram_tensor("out_0", (P, TILES, DM), F32, kind="ExternalOutput").ap())
    two_layers(nc, *args)
    r = _run(nc, [{f"in_{n}": v for n, v in arrays.items()}], core_ids=[0])
    got = np.asarray(r.results[0]["out_0"])
    return np.ascontiguousarray(got.transpose(1, 0, 2)).reshape(BATCH, SEQ, DM)
```

```python
from contextlib import ExitStack

import numpy as np

import concourse.bass as bass
from concourse import mybir

P = 128
BATCH, SEQ, DM = 2, 512, 256
TILES = BATCH * SEQ // P
TPB = SEQ // P
CH = DM // P
HEADS, HD = 16, 16
HPG = 4
GROUPS = BATCH * HEADS // HPG
GW = 3 * HPG * HD
SLOT = 64
EXPERTS, TOPK, INTER = 16, 4, 128
NGRP, GSZ = 4, 4
FFN_INTER = 704
FFN_CHUNKS = -(-FFN_INTER // P)
STREAM = 1 + EXPERTS + FFN_CHUNKS
WCOLS = 2 * CH * P + DM
SCALE = HD ** -0.5
EPS = 1e-5
NEG = -1e30

F32 = mybir.dt.float32
F32R = mybir.dt.float32r
BF16 = mybir.dt.bfloat16
ACT = mybir.ActivationFunctionType
ALU = mybir.AluOpType
AX = mybir.AxisListType
ds = bass.ds

BANK_S1, BANK_S2, BANK_O, BANK_T = (0, 1), (2, 3), 4, (5, 6, 7)
BANK_G, BANK_U, BANK_Y = (0, 1), (2, 3), (4, 5, 6, 7)
BANK_NORM = (4, 6, 1, 3)
CTX_FILLS = ((0, 0), (1, 0), (0, 1), (1, 1))
BANK_CTX = (0, 1, 5, 6)
BANK_PROJ = (2, 3, 0, 1)
BANK_LT, BANK_LOGITS = (4, 6), 5

VALUES_AT = ((6, 9, 13), (7, 11, 15))
NEXT_TURNS_AT = (14, 14)
SPLIT_AT = ((7, 9), (7, 9))

WARM_START, WARM_FIRST_STEP, WARM_BETWEEN = 14, (9, 5), 8
BANK_WARM = 0


def two_layers(nc, x, wqkv, bqkv, wo, bo, rope, mask, ident_in, router_w, router_b, ties, stream_w,
               stream_scale, down_scale, out):
    with ExitStack() as ctx:
        def sb(name, shape, dt=F32):
            return ctx.enter_context(nc.sbuf_tensor(name, shape, dt))

        def sem(name):
            return ctx.enter_context(nc.semaphore(name))

        X = sb("resid", [P, TILES, DM])
        XN = sb("normed", [P, TILES, DM])
        XT = [sb(f"xT_{n}", [P, CH, BATCH * SEQ], F32R) for n in ("hi", "lo")]
        stage_qkv = sb("stage_qkv", [P, CH, 3 * DM])
        WQKV = [sb(f"wqkv_{n}", [P, CH, 3 * DM], F32R) for n in ("hi", "lo")]
        stage_wo = sb("stage_wo", [P, CH, DM])
        WO = [sb(f"wo_{n}", [P, CH, DM], F32R) for n in ("hi", "lo")]
        BQKV = sb("b_qkv", [P, 3 * DM])
        BO = sb("b_o", [P, DM])
        ROPE = sb("rope_tables", [P, 2, TPB * HPG, HD])
        ident = sb("ident", [P, P])
        ident_r = sb("ident_r", [P, P], F32R)
        MASK = sb("causal_mask", [P, SEQ])
        masked = sb("masked_scores", [P, 2, SEQ])
        QKV = [sb(f"qkv{s}", [P, 3, TPB * HPG, HD]) for s in range(2)]
        QK = [q[:, 0:2] for q in QKV]
        ROT = sb("rotated", [P, 2, TPB * HPG, HD])
        ROPED = [sb(f"roped{s}", [P, 2, TPB * HPG, HD]) for s in range(2)]
        QS = [sb(f"q_stack{s}", [P, TPB * HPG, SLOT], F32R) for s in range(2)]
        KS = [sb(f"k_stack{s}", [P, TPB * HPG, SLOT], F32R) for s in range(2)]
        QT = [sb(f"qT{s}", [P, 2, SEQ], F32R) for s in range(2)]
        KT = [sb(f"kT{s}", [P, HPG, SEQ], F32R) for s in range(2)]
        VS = [sb(f"v_stack{s}", [P, TPB, HPG, 32]) for s in range(2)]
        NRING = 8
        PT = sb("probsT", [P, NRING, SEQ])
        OS = sb("outT", [P, SEQ])
        MX = [sb(f"maxes{s}", [P, HPG, TPB]) for s in range(2)]
        RD = sb("rdenom", [P, TPB * HPG])
        STATS = sb("bn_stats", [P, TILES, 6])
        MV = sb("mean_var", [P, TILES, 2])
        VE = sb("var_eps", [P, TILES])
        SD = sb("std", [P, TILES])
        RSTD = sb("rstd", [P, TILES])
        stage_w = [sb(f"stage_w{s}", [P, WCOLS]) for s in range(2)]
        WE = [[sb(f"we_{n}{s}", [P, WCOLS], F32R) for n in ("hi", "lo")] for s in range(4)]
        SG = [PT[:, s, :] for s in range(2)]
        HF = [PT[:, 2 + s, :] for s in range(2)]
        HR = [[sb(f"h_{n}{s}", [P, SEQ], F32R) for n in ("hi", "lo")] for s in range(4)]
        SSC = sb("stream_scale", [P, FFN_CHUNKS, 2])
        DSC = sb("down_scale", [P, DM])
        LT = PT[0:EXPERTS, 4:6, :]
        CMP = [PT[:, 2 * s + 4:2 * s + 6, :].bitcast(BF16).rearrange("p a (b c) -> p (a b) c", c=EXPERTS) for s in range(2)]
        TIEB = sb("ties_bf16", [P, EXPERTS, EXPERTS], BF16)
        GWS = sb("router_stage", [P, CH, EXPERTS])
        GWT = [sb(f"router_{n}", [P, CH, EXPERTS], F32R) for n in ("hi", "lo")]
        EB = sb("router_bias", [P, EXPERTS])
        TIES = sb("ties", [P, EXPERTS, EXPERTS])
        TIEG = sb("ties_groups", [P, NGRP, NGRP])
        R = {n: sb(f"route_{n}", [P, TILES, EXPERTS]) for n in ("e", "s", "b", "v", "gm", "w", "c")}
        RG = {n: sb(f"rgrp_{n}", [P, TILES, NGRP, w]) for n, w in (("hi", 2), ("lo", 2), ("t1", 1), ("a", 1), ("b", 1), ("s", 1))}
        RK = sb("rank", [P, TILES, EXPERTS])
        RKG = sb("rank_g", [P, TILES, NGRP])
        CG = sb("cmp_g", [P, 2, TILES, NGRP, NGRP])
        WSUM = sb("wsum", [P, TILES])
        WREC = sb("wrec", [P, TILES])

        PS = ctx.enter_context(nc.psum_tensor("psum", [P, 8, 512], F32))

        x_in = [sem(f"x_in{half}") for half in range(2)]
        rows_in, tables_in = sem("rows_in"), sem("tables_in")
        ident_loaded, rope_in = sem("ident_loaded"), sem("rope_in")
        ident_r_ready = sem("ident_r_ready")
        wqkv_in, wo_in = sem("wqkv_in"), sem("wo_in")
        stream_in = [sem(f"stream_in{s}") for s in range(2)]
        zeroed = sem("zeroed")
        consts_ready = sem("consts_ready")
        out_stored = sem("out_stored")
        dve_self = sem("dve_self")
        pool_self = sem("pool_self")
        var_ready, std_ready, normed = sem("var_ready"), sem("std_ready"), sem("normed")
        xT_ready, xT_hi_done, xT_lo_done = sem("xT_ready"), sem("xT_hi_done"), sem("xT_lo_done")
        wsplit_hi, wsplit_lo = sem("wsplit_hi"), sem("wsplit_lo")
        bias_added = sem("bias_added")
        proj_out_ready, resid_done = sem("proj_out_ready"), sem("resid_done")
        qkv_ready, qkv_taken = sem("qkv_ready"), sem("qkv_taken")
        rope_part, rope_done = sem("rope_part"), sem("rope_done")
        stack_hi, stack_lo = sem("stack_hi"), sem("stack_lo")
        v_stacked = sem("v_stacked")
        qT_ready, qT_taken = sem("qT_ready"), sem("qT_taken")
        kT_ready, kT_taken = sem("kT_ready"), sem("kT_taken")
        s1_ready, s1_reduced = sem("s1_ready"), sem("s1_reduced")
        m_hi, m_lo = sem("m_hi"), sem("m_lo")
        mT_ready, mT_taken = sem("mT_ready"), sem("mT_taken")
        s2_ready, exp_done, probs_masked = sem("s2_ready"), sem("exp_done"), sem("probs_masked")
        pv_done, o_taken = sem("pv_done"), sem("o_taken")
        oT_ready, rd_done, ctx_done = sem("oT_ready"), sem("rd_done"), sem("ctx_done")
        we_hi, we_lo = sem("we_hi"), sem("we_lo")
        gu_ready, silu_done, h_done = sem("gu_ready"), sem("silu_done"), sem("h_done")
        h_hi, h_lo = sem("h_hi"), sem("h_lo")
        y_ready, y_added = sem("y_ready"), sem("y_added")
        lT_ready, lT_taken = sem("logitsT_ready"), sem("logitsT_taken")
        logits_ready, router_exp, routed = sem("logits_ready"), sem("router_exp"), sem("routed")
        out_scaled, out_ready, out_ready_even = sem("out_scaled"), sem("out_ready_odd"), sem("out_ready_even")

        block = ctx.enter_context(nc.Block())

        def need(eng, s, value):
            if not isinstance(value, int) or value > 0:
                eng.wait_ge(s, value)

        class Steps:

            def __init__(self, s):
                self.s, self.n = s, 0

            def done(self, ins):
                self.n += 1
                return ins.then_inc(self.s, 1)

        def in_layer(c, d):
            return 0 <= c + d < GROUPS

        def rope_cos(s, rows):
            width = (rows.stop - rows.start) * HD
            cos = ROPE[:, 0, rows, :].rearrange("p r d -> p (r d)").unsqueeze(1).broadcast_to([P, 2, width])
            flat = [w[:, :, rows, :].rearrange("p a r d -> p a (r d)") for w in (ROPED[s], QK[s])]
            return flat[0], flat[1], cos, ALU.mult

        def rope_sin(s, rows, j):
            d, o = slice(8 * j, 8 * j + 8), slice(8 - 8 * j, 16 - 8 * j)
            sin = ROPE[:, 1, rows, d].unsqueeze(1).broadcast_to([P, 2, rows.stop - rows.start, 8])
            return ROT[:, :, rows, d], QK[s][:, :, rows, o], sin, ALU.mult

        def rope_sum(s, rows):
            return ROPED[s][:, :, rows, :], ROPED[s][:, :, rows, :], ROT[:, :, rows, :], ALU.add

        def q_lo(layer, s):
            src = QK[s] if layer else ROPED[s]
            return QS[s][:, :, 2 * HD:3 * HD], src[:, 0], QS[s][:, :, 0:HD].bitcast(F32), ALU.subtract

        def k_lo(layer, s):
            src = QK[s] if layer else ROPED[s]
            return KS[s][:, :, HD:2 * HD], src[:, 1], KS[s][:, :, 0:HD].bitcast(F32), ALU.subtract

        @block.sync
        def _(sp):
            def load(dst, src, s):
                sp.dma_start(dst, src).then_inc(s, 16)

            load(ident[:, :], ident_in, ident_loaded)
            for t in range(0, TILES, TPB):
                load(X[:, t:t + 4, :], x[:, t:t + 4, :], x_in[t // TPB])
            load(stage_qkv[:, :, :], wqkv[0], wqkv_in)
            load(BQKV[:, :], bqkv[0].partition_broadcast(P), rows_in)
            load(BO[:, :], bo[0].partition_broadcast(P), rows_in)
            load(ROPE[:, :, :, :], rope, rope_in)
            load(stage_wo[:, :, :], wo[0], wo_in)
            load(MASK[:, :], mask, tables_in)
            load(GWS[:, :, :], router_w, tables_in)
            load(EB[:, :], router_b.partition_broadcast(P), tables_in)
            load(TIES[:, :, :].rearrange("p a b -> p (a b)"), ties[0:1, 0:256].rearrange("a b -> (a b)").partition_broadcast(P), tables_in)
            load(TIEG[:, :, :].rearrange("p a b -> p (a b)"), ties[0:1, 256:272].rearrange("a b -> (a b)").partition_broadcast(P), tables_in)
            load(SSC[:, :, :], stream_scale, tables_in)
            load(DSC[:, :], down_scale.partition_broadcast(P), tables_in)
            for e in range(2):
                load(stage_w[e][:, :], stream_w[e], stream_in[e])
            need(sp, wsplit_lo, 1)
            load(stage_qkv[:, :, :], wqkv[1], wqkv_in)
            need(sp, wsplit_lo, 2)
            load(stage_wo[:, :, :], wo[1], wo_in)
            need(sp, qkv_taken, 4 * GROUPS)
            load(BQKV[:, :], bqkv[1].partition_broadcast(P), rows_in)
            need(sp, bias_added, 1)
            load(BO[:, :], bo[1].partition_broadcast(P), rows_in)

            def load_expert(i, c):
                sp.wait_ge(we_hi, 4 * i + c - 1)
                sp.wait_ge(we_lo, 4 * i + c - 1)
                load(stage_w[c % 2][:, :], stream_w[ds(4 * i + c, 1)].rearrange("e p w -> (e p) w"), stream_in[c % 2])

            with sp.Fori(0, 5) as i:
                for c in range(2, 6):
                    load_expert(i, c)
            load_expert(0, STREAM - 1)
            for half in range(2):
                for j in range(2):
                    for t, ready in ((0, out_ready_even), (1, out_ready)):
                        tile = half * TPB + 2 * j + t
                        sp.wait_ge(ready, tile // 2 + 1)
                        sp.dma_start(out[:, tile, :], X[:, tile, :]).then_inc(out_stored, 16)
            sp.wait_ge(out_stored, 16 * TILES)

        @block.tensor
        def _(pe):
            def product(dst, left, right, start=True, stop=True, skip=False):
                pe.matmul(dst, left[0], right[0], start=start, stop=False, skip_group_check=skip)
                pe.matmul(dst, left[0], right[1], start=False, stop=False, skip_group_check=skip)
                return pe.matmul(dst, left[1], right[0], start=False, stop=stop, skip_group_check=skip)

            def to_features(fill, bank):
                half, c = fill
                for t in range(TPB):
                    mm = pe.transpose(PS[:, bank, t * P:(t + 1) * P],
                                      XN[:, half * TPB + t, c * P:(c + 1) * P], ident[:, :])
                mm.then_inc(xT_ready, 1)

            def norm_to_features(l, half):
                pe.wait_ge(normed, 2 * l + half + 1)
                for c in range(CH):
                    to_features((half, c), BANK_NORM[2 * half + c])

            def context_to_features(layer, f):
                half, c = CTX_FILLS[f]
                pe.wait_ge(ctx_done, GROUPS * layer + (3, 4, 7, 8)[f])
                to_features((half, c), BANK_CTX[f])

            def features_there(n):
                pe.wait_ge(xT_hi_done, n)
                pe.wait_ge(xT_lo_done, n)

            def project_out(layer, t):
                if t % TPB == 0:
                    features_there(12 * layer + (7, 8)[t // TPB])
                    pe.wait_ge(wsplit_lo, 2 * layer + 2)
                need(pe, resid_done, TILES * layer + t - 3 if t >= 4 else 0)
                for c in range(CH):
                    mm = product(PS[:, BANK_PROJ[t % 4], 0:DM], [w[:, c, t * P:(t + 1) * P] for w in XT],
                                 [w[:, c, :] for w in WO], start=(c == 0), stop=(c == CH - 1))
                mm.then_inc(proj_out_ready, 1)

            def attention_step(layer, m, c):
                s0, s1 = c % 2, (c + 1) % 2
                has_c, has_b, has_a, has_o = (in_layer(c, d) for d in (0, 1, 2, -1))

                def project(unit, j):
                    g = m + 2
                    if j == 0 and unit == 0:
                        if has_b:
                            pe.wait_ge(qT_taken, 2 * m + 3)
                        features_there(12 * layer + (2 if c == -2 else 4))
                        pe.wait_ge(wsplit_lo, 2 * layer + 1)
                    if j == 0 and unit == 1:
                        need(pe, mT_taken, 2 * m + 2)
                        need(pe, qkv_taken, 4 * g)
                    col = GW * ((g - GROUPS * layer) // 2) if isinstance(g, int) else (c + 2) // 2 * GW + (m - c - GROUPS * layer) * (GW // 2)
                    t = 4 * s0 + 2 * unit + j
                    for k in range(CH):
                        mm = product(PS[:, BANK_T[2 * unit], j * GW:(j + 1) * GW],
                                     [w[:, k, t * P:(t + 1) * P] for w in XT],
                                     [w[:, k, ds(col, GW)] for w in WQKV], start=(k == 0), stop=(k == CH - 1))
                    if j == 1:
                        mm.then_inc(qkv_ready, 1)

                def turn(stack, p, bank, ready):
                    for t in range(TPB):
                        mm = pe.transpose(PS[:, bank, t * P:(t + 1) * P].bitcast(F32R),
                                          stack[:, t * HPG + 2 * p:t * HPG + 2 * p + 2, :].rearrange("p h w -> p (h w)"),
                                          ident_r[:, :])
                    mm.then_inc(ready, 1)

                def scores(u):
                    g, h, qt = m + 1, u // TPB, u % TPB
                    keys = P * (qt + 1) if layer else SEQ
                    if u in (0, 8):
                        pe.wait_ge(qT_taken, 2 * g + u // 8 + 1)
                    if u % TPB == 0:
                        pe.wait_ge(kT_taken, 4 * g + h + 1)
                    need(pe, s1_reduced, 16 * g + u - 1)
                    bank = BANK_S1[u % 2]
                    mm = pe.matmul(PS[:, bank, 0:keys], QT[s1][:, h // 2, qt * P:(qt + 1) * P],
                                   KT[s1][:, h, 0:keys], start=True, stop=True)
                    mm.then_inc(s1_ready, 1)

                def scores_t(u):
                    kt, h = u // HPG, u % HPG
                    q0 = P * kt if layer else 0
                    if u in (0, 2):
                        pe.wait_ge(mT_taken, 2 * m + 1 + u // 2)
                    need(pe, exp_done, 16 * m + u - 1)
                    bank = BANK_S2[u % 2]
                    mm = pe.matmul(PS[:, bank, q0:SEQ], KT[s0][:, h, kt * P:(kt + 1) * P],
                                   QT[s0][:, h // 2, q0:SEQ], start=True, stop=True)
                    mm.then_inc(s2_ready, 1)

                def values(m, s0, kt):
                    q0 = P * kt if layer else 0
                    pe.wait_ge(exp_done, 16 * m + 4 * kt + 4)
                    if layer:
                        pe.wait_ge(probs_masked, 4 * (m - GROUPS) + kt + 1)
                    if kt == 0:
                        need(pe, o_taken, m)
                        pe.wait_ge(v_stacked, m + 1)
                    for h in range(HPG):
                        mm = pe.matmul(PS[32 * h:32 * h + 32, BANK_O, q0:SEQ], VS[s0][:, kt, h, :],
                                       PT[:, (4 * kt + h) % NRING, q0:SEQ], start=(kt == 0),
                                       stop=(kt == TPB - 1), skip_group_check=True)
                    mm.then_inc(pv_done, 1)

                for u in range(4 * TPB):
                    if has_c and u < 2:
                        scores_t(u)
                    if has_c and u == 1:
                        pe.wait_ge(m_lo, 2 * m + 2)
                        pe.wait_ge(mT_taken, 2 * m + 1)
                        turn(QS[s0], 1, BANK_T[2], mT_ready)
                    if has_b:
                        scores(u)
                    if has_c and u > 2:
                        scores_t(u)
                    if has_a and u in (0, 1):
                        project(0, u)
                    if has_o and u == 2:
                        values(m - 1, s1, TPB - 1)
                    if has_c and u == 2:
                        scores_t(u)
                    if has_b and u == 2:
                        need(pe, ident_r_ready, 1)
                        pe.wait_ge(kT_taken, 4 * m + 6)
                        turn(QS[s1], 1, BANK_T[1], qT_ready)
                    if has_a and u in (3, 4):
                        project(1, u - 3)
                    if c == -2 and u == 5:
                        keep_warm(WARM_FIRST_STEP[layer])
                    if has_b and u == 5:
                        if has_a:
                            pe.wait_ge(qkv_taken, 4 * m + 10)
                        turn(KS[s1], 1, BANK_T[0], kT_ready)
                    if has_o and u == 5:
                        pe.wait_ge(o_taken, m)
                        if has_b:
                            pe.wait_ge(qT_taken, 2 * m + 4)
                        turn_output(BANK_T[1])
                    if has_a and u == NEXT_TURNS_AT[layer]:
                        pe.wait_ge(stack_lo, 3 * m + 9)
                        if has_b:
                            pe.wait_ge(kT_taken, 4 * m + 8)
                        turn(QS[s0], 0, BANK_T[0], qT_ready)
                        need(pe, ctx_done, m)
                        turn(KS[s0], 0, BANK_T[1], kT_ready)
                    if has_c and u in VALUES_AT[layer]:
                        values(m, s0, VALUES_AT[layer].index(u))
                    if c == -2 and u == 15:
                        norm_to_features(2 * layer, 1)
                    if c == GROUPS - 1 and u in (2, 3, 12):
                        context_to_features(layer, (2, 3, 12).index(u))
                    if has_b and u == 11:
                        pe.wait_ge(m_lo, 2 * m + 3)
                        if has_a:
                            pe.wait_ge(qkv_taken, 4 * m + 12)
                        turn(QS[s1], 0, BANK_T[2], mT_ready)
                if c == GROUPS - 1:
                    values(m, s0, TPB - 1)

            def turn_output(bank):
                for t in range(TPB):
                    mm = pe.transpose(PS[:, bank, t * P:(t + 1) * P], OS[:, t * P:(t + 1) * P], ident[:, :])
                mm.then_inc(oT_ready, 1)

            def attention(layer):
                base = GROUPS * layer
                for c in range(-2, GROUPS):
                    attention_step(layer, base + c, c)
                project_out(layer, 0)
                pe.wait_ge(o_taken, base + GROUPS)
                turn_output(BANK_T[2])
                project_out(layer, 1)
                context_to_features(layer, 3)
                project_out(layer, 2)
                project_out(layer, 3)
                for t in range(TPB, TILES):
                    project_out(layer, t)

            def gate_up(i, c, half):
                e = 4 * i + c
                k = 2 * e + half
                if half == 0:
                    pe.wait_ge(we_lo, e + 1)
                need(pe, h_done, k - 1 if not isinstance(k, int) or k >= 2 else 0)
                W = WE[c % 4]
                for bank, w0 in ((BANK_G[half], 0), (BANK_U[half], CH * P)):
                    for j in range(CH):
                        mm = product(PS[:, bank, :], [w[:, w0 + j * P:w0 + (j + 1) * P] for w in W],
                                     [w[:, j, half * SEQ:(half + 1) * SEQ] for w in XT],
                                     start=(j == 0), stop=(j == CH - 1))
                mm.then_inc(gu_ready, 1)

            def down_sum(c, half):
                k = 2 * c + half
                pe.wait_ge(h_lo, k + 1)
                W, H = WE[c % 4], HR[k % 4]
                for t in range(TPB):
                    tile = TPB * half + t
                    mm = product(PS[:, BANK_Y[tile // 2], tile % 2 * DM:(tile % 2 + 1) * DM],
                                 [w[:, t * P:(t + 1) * P] for w in H], [w[:, 2 * CH * P:] for w in W],
                                 start=(c == STREAM - FFN_CHUNKS and t % 2 == 0), stop=(c == STREAM - 1), skip=True)
                    if c == STREAM - 1 or t == TPB - 1:
                        mm.then_inc(y_ready, 1 if c == STREAM - 1 else 4)

            def down(i, c, half):
                k = 8 * i + 2 * c + half
                pe.wait_ge(h_lo, k + 1)
                W, H = WE[c % 4], HR[(2 * c + half) % 4]
                for t in range(TPB):
                    need(pe, y_added, 4 * k + t - 3 if not isinstance(k, int) or k else 0)
                    product(PS[:, BANK_Y[t], 0:DM], [w[:, t * P:(t + 1) * P] for w in H],
                            [w[:, 2 * CH * P:] for w in W]).then_inc(y_ready, 1)

            def router_logits(half):
                features_there(10 + 2 * half)
                cols = slice(half * SEQ, (half + 1) * SEQ)
                for c in range(CH):
                    mm = product(PS[0:EXPERTS, BANK_LT[half], :], [w[:, c, :] for w in GWT],
                                 [w[:, c, cols] for w in XT], start=(c == 0), stop=(c == CH - 1))
                mm.then_inc(lT_ready, 1)

            def turn_logits():
                pe.wait_ge(lT_taken, 2)
                for t in range(TILES):
                    mm = pe.transpose(PS[:, BANK_LOGITS, t * EXPERTS:(t + 1) * EXPERTS],
                                      LT[:, t // TPB, t % TPB * P:(t % TPB + 1) * P],
                                      ident[0:EXPERTS, 0:EXPERTS])
                mm.then_inc(logits_ready, 1)

            def keep_warm(n):
                with pe.Fori(0, n):
                    for _ in range(4):
                        pe.transpose(PS[:, BANK_WARM, 0:P], ident[:, :], ident[:, :])

            def units(pairs):
                for i, c in pairs:
                    for half in range(2):
                        gate_up(i, c, half)
                        down(i, c - 1, half)

            pe.wait_ge(ident_loaded, 16)
            keep_warm(WARM_START)
            for layer in range(2):
                norm_to_features(2 * layer, 0)
                attention(layer)
                norm_to_features(2 * layer + 1, 0)
                if layer == 0:
                    pe.wait_ge(consts_ready, 2)
                    router_logits(0)
                    gate_up(0, 0, 0)
                    norm_to_features(1, 1)
                    router_logits(1)
                    turn_logits()
                    gate_up(0, 0, 1)
                    pe.wait_ge(router_exp, 1)
                    units([(0, 1)])
                    with pe.Fori(0, 3) as i:
                        units((i, c) for c in range(2, 6))
                    units((0, c) for c in range(14, 1 + EXPERTS))
                    for half in range(2):
                        down(0, EXPERTS, half)
                    keep_warm(WARM_BETWEEN)
                else:
                    features_there(22)
                    gate_up(0, 17, 0)
                    norm_to_features(3, 1)
                    features_there(24)
                    gate_up(0, 17, 1)
                    for c in range(18, STREAM):
                        for half in range(2):
                            gate_up(0, c, half)
                            down_sum(c - 1, half)
                    for half in range(2):
                        down_sum(STREAM - 1, half)

        @block.vector
        def _(dve):
            own = Steps(dve_self)

            def after_own():
                dve.wait_ge(dve_self, own.n)

            def statistics(t):
                own.done(dve.bn_stats(STATS[:, t, :], X[:, t, :]))

            def variances(half):
                after_own()
                tiles = slice(TPB * half, TPB * (half + 1))
                for t in range(TPB * half, TPB * (half + 1)):
                    own.done(dve.bn_aggr(MV[:, t, :], STATS[:, t, :]))
                after_own()
                dve.tensor_scalar(VE[:, tiles], MV[:, tiles, 1], EPS, None, ALU.add).then_inc(var_ready, 1)

            def normalise(l, half):
                tiles = slice(TPB * half, TPB * (half + 1))
                dve.wait_ge(std_ready, 2 * l + half + 1)
                own.done(dve.reciprocal(RSTD[:, tiles], SD[:, tiles]))
                after_own()
                for t in range(TPB * half, TPB * (half + 1)):
                    ins = dve.tensor_scalar(XN[:, t, :], X[:, t, :], MV[:, t, 0:1], RSTD[:, t:t + 1],
                                            ALU.subtract, ALU.mult)
                ins.then_inc(normed, 1)

            def take_lo(n, fill, bank):
                half, c = fill
                cols = slice(half * SEQ, (half + 1) * SEQ)
                dve.wait_ge(xT_hi_done, n + 1)
                dve.tensor_tensor(XT[1][:, c, cols], PS[:, bank, :], XT[0][:, c, cols].bitcast(F32),
                                  ALU.subtract).then_inc(xT_lo_done, 1)

            def norm_lo(l, half):
                n = (0, 8, 12, 20)[l] + 2 * half
                for c in range(CH):
                    take_lo(n + c, (half, c), BANK_NORM[2 * half + c])

            def context_both(layer, f):
                half, c = CTX_FILLS[f]
                n = 12 * layer + 4 + f
                dve.wait_ge(xT_ready, n + 1)
                dve.tensor_copy(XT[0][:, c, half * SEQ:(half + 1) * SEQ],
                                PS[:, BANK_CTX[f], :]).then_inc(xT_hi_done, 1)
                take_lo(n, (half, c), BANK_CTX[f])

            def split_weights(n):
                dst, src = ((WQKV, stage_qkv), (WO, stage_wo))[n]
                dve.wait_ge(wsplit_hi, n + 1)
                dve.tensor_tensor(dst[1][:, :, :], src[:, :, :], dst[0][:, :, :].bitcast(F32),
                                  ALU.subtract).then_inc(wsplit_lo, 1)

            def attention_step(layer, m, c):
                s0, s1 = c % 2, (c + 1) % 2
                has_c, has_b, has_a, has_o = (in_layer(c, d) for d in (0, 1, 2, -1))

                def take_qkv(unit):
                    g = m + 2
                    dve.wait_ge(qkv_ready, 2 * g + unit + 1)
                    if unit == 0:
                        need(dve, stack_lo, 3 * g - 3)
                        need(dve, stack_hi, 2 * g - 2)
                        need(dve, v_stacked, g - 1)
                        if layer == 0:
                            need(dve, rope_part, 6 * g - 6)
                    if c == -2 and unit == 0:
                        dve.wait_ge(rows_in, 32 * (layer + 1))
                        dve.wait_ge(zeroed, 1)
                    col = GW * ((g - GROUPS * layer) // 2) if isinstance(g, int) else (c + 2) // 2 * GW + (m - c - GROUPS * layer) * (GW // 2)
                    got = PS[:, BANK_T[2 * unit], 0:2 * GW].rearrange("p (t w) -> p t w", t=2)
                    rows = slice(2 * HPG * unit, 2 * HPG * (unit + 1))
                    bias = BQKV[:, ds(col, GW)].rearrange("p (a w) -> p a w", a=3).unsqueeze(2)
                    dve.tensor_tensor(QKV[s0][:, :, rows, :].rearrange("p a (t h) d -> p a t (h d)", t=2),
                                      got.rearrange("p t (a w) -> p a t w", a=3),
                                      bias.broadcast_to([P, 3, 2, HPG * HD]), ALU.add).then_inc(qkv_taken, 2)

                def rope(unit):
                    rows = slice(2 * HPG * unit, 2 * HPG * (unit + 1))
                    if unit == 0:
                        dve.wait_ge(rope_in, 16)
                    dve.wait_ge(qkv_taken, 2 * unit + 2)
                    need(dve, rope_done, unit)
                    dve.tensor_tensor(*rope_cos(s0, rows)).then_inc(rope_part, 1)
                    for j in range(2):
                        dve.tensor_tensor(*rope_sin(s0, rows, j)).then_inc(rope_part, 1)
                    dve.wait_ge(rope_part, 3 * unit + 3)
                    dve.tensor_tensor(*rope_sum(s0, rows)).then_inc(rope_done, 1)

                def split_lo():
                    g = m + 2
                    dve.wait_ge(stack_hi, 2 * g + 2)
                    dve.memset(QS[s0][:, :, 3 * HD:3 * HD + 2].bitcast(F32), 0.0).then_inc(stack_lo, 1)
                    dve.tensor_tensor(*q_lo(layer, s0)).then_inc(stack_lo, 1)
                    dve.tensor_tensor(*k_lo(layer, s0)).then_inc(stack_lo, 1)

                def take_qT(g, s, p):
                    dve.wait_ge(qT_ready, 2 * g + p + 1)
                    if p == 0:
                        need(dve, s2_ready, 16 * g - 18)
                    dve.tensor_copy(QT[s][:, p, :], PS[:, BANK_T[p], :]).then_inc(qT_taken, 1)

                def reduce(u):
                    g, h, qt = m + 1, u // TPB, u % TPB
                    keys = P * (qt + 1) if layer else SEQ
                    dve.wait_ge(s1_ready, 16 * g + u + 1)
                    if layer == 0:
                        dve.tensor_reduce(MX[s1][:, h, qt:qt + 1], PS[:, BANK_S1[u % 2], 0:keys], AX.X,
                                          ALU.max).then_inc(s1_reduced, 1)
                    else:
                        if u == 0:
                            need(dve, tables_in, 16 * 7)
                        dve.wait_ge(s1_reduced, 16 * g + u - 1)
                        dve.tensor_tensor_reduce(out=masked[:, u % 2, 0:keys], in0=PS[:, BANK_S1[u % 2], 0:keys],
                                                 in1=MASK[:, SEQ - keys:SEQ], scale=1.0, scalar=NEG,
                                                 op0=ALU.add, op1=ALU.max,
                                                 accum_out=MX[s1][:, h, qt:qt + 1]).then_inc(s1_reduced, 1)

                def split_max(p):
                    g = m + 1
                    dve.wait_ge(s1_reduced, 16 * g + 8 * p + 8)
                    stack = QS[s1][:, :, :].rearrange("p (t h) w -> p t h w", t=TPB)
                    mx = MX[s1][:, 2 * p:2 * p + 2, :].rearrange("p h t -> p t h")
                    hi = stack[:, :, 2 * p:2 * p + 2, 3 * HD]
                    lo = stack[:, :, 2 * p:2 * p + 2, 3 * HD + 1]
                    dve.tensor_scalar(hi, mx, -1.0, None, ALU.mult).then_inc(m_hi, 1)
                    dve.wait_ge(m_hi, 2 * g + p + 1)
                    dve.scalar_tensor_tensor(lo, mx, -1.0, hi.bitcast(F32), ALU.mult,
                                             ALU.subtract).then_inc(m_lo, 1)

                for u in range(4 * TPB):
                    if has_b:
                        reduce(u)
                    if has_a and u in (1, 5):
                        take_qkv(u // 4)
                    if c == -2 and u == 6:
                        if layer == 0:
                            for unit in range(2):
                                rope(unit)
                        normalise(2 * layer, 1)
                        split_lo()
                    if c == GROUPS - 1 and u in (2, 3, 12):
                        context_both(layer, (2, 3, 12).index(u))
                    if has_b and u == 3:
                        take_qT(m + 1, s1, 1)
                    if has_b and u == 8:
                        split_max(0)
                    if has_o and u == 9:
                        normalise_context(layer, m - 1, c - 1, BANK_T[1])
                    if has_a and u == NEXT_TURNS_AT[layer]:
                        take_qT(m + 2, s0, 0)
                if has_b:
                    split_max(1)
                if c == -2:
                    norm_lo(2 * layer, 1)
                    if layer == 0:
                        split_weights(1)

            def normalise_context(layer, m, c, bank):
                T = PS[:, bank, :].rearrange("p (r w) -> p r w", w=32)
                dve.wait_ge(oT_ready, m + 1)
                dve.reciprocal(RD[:, :], T[:, :, HD]).then_inc(rd_done, 1)
                dve.wait_ge(rd_done, m + 1)
                t0 = TPB * (c % 2)
                col = HPG * HD * (c // 2) if isinstance(m, int) else (m - c - GROUPS * layer) * (HPG * HD // 2) + c // 2 * HPG * HD
                dst = XN[:, t0:t0 + TPB, ds(col, HPG * HD)].rearrange("p t (h d) -> p t h d", h=HPG)
                src = T[:, :, 0:HD].rearrange("p (t h) d -> p t h d", t=TPB)
                rd = RD[:, :].rearrange("p (t h) -> p t h", t=TPB).unsqueeze(3).broadcast_to([P, TPB, HPG, HD])
                dve.tensor_tensor(dst, src, rd, ALU.mult).then_inc(ctx_done, 1)

            def attention(layer):
                base = GROUPS * layer
                for c in range(-2, GROUPS):
                    attention_step(layer, base + c, c)
                residual(layer, 0)
                normalise_context(layer, base + GROUPS - 1, GROUPS - 1, BANK_T[2])
                residual(layer, 1)
                residual(layer, 2)
                take_lo(12 * layer + 7, CTX_FILLS[3], BANK_CTX[3])
                residual(layer, 3)
                statistics_of(layer, range(TPB))
                variances(0)
                residual(layer, 4)
                residual(layer, 5)
                normalise(2 * layer + 1, 0)
                residual(layer, 6)
                residual(layer, 7)
                norm_lo(2 * layer + 1, 0)
                statistics_of(layer, range(TPB, TILES))
                variances(1)
                normalise(2 * layer + 1, 1)
                norm_lo(2 * layer + 1, 1)

            def residual(layer, t):
                dve.wait_ge(proj_out_ready, TILES * layer + t + 1)
                if t == 0:
                    dve.wait_ge(bias_added, layer + 1)
                dve.tensor_tensor(X[:, t, :], PS[:, BANK_PROJ[t % 4], 0:DM], X[:, t, :],
                                  ALU.add).then_inc(resid_done, 1)

            def statistics_of(layer, tiles):
                dve.wait_ge(resid_done, TILES * layer + tiles[-1] + 1)
                for t in tiles:
                    statistics(t)

            def step(ins):
                own.done(ins)
                after_own()

            sc = R["e"]

            def router_groups():
                dve.wait_ge(tables_in, 16 * 7)
                own.done(dve.tensor_copy(TIEB[:, :, :], TIES[:, :, :]))
                dve.wait_ge(router_exp, 1)
                step(dve.tensor_scalar(R["s"][:, :, :], R["e"][:, :, :], 1.0, None, ALU.add))
                step(dve.reciprocal(R["e"][:, :, :], R["s"][:, :, :]))
                step(dve.tensor_tensor(R["b"][:, :, :], sc[:, :, :],
                                       EB[:, :].unsqueeze(1).broadcast_to([P, TILES, EXPERTS]), ALU.add))
                b4 = R["b"][:, :, :].rearrange("p t (g a c) -> p (t g) a c", g=NGRP, a=2)
                fl = {n: v[:, :, :, :].rearrange("p t g w -> p (t g) w") for n, v in RG.items()}
                own.done(dve.tensor_tensor(fl["hi"][:, :, :], b4[:, :, :, 0], b4[:, :, :, 1], ALU.max))
                step(dve.tensor_tensor(fl["lo"][:, :, :], b4[:, :, :, 0], b4[:, :, :, 1], ALU.min))
                own.done(dve.tensor_tensor(fl["t1"][:, :, :], fl["hi"][:, :, 0:1], fl["hi"][:, :, 1:2], ALU.max))
                own.done(dve.tensor_tensor(fl["a"][:, :, :], fl["hi"][:, :, 0:1], fl["hi"][:, :, 1:2], ALU.min))
                step(dve.tensor_tensor(fl["b"][:, :, :], fl["lo"][:, :, 0:1], fl["lo"][:, :, 1:2], ALU.max))
                step(dve.tensor_tensor(fl["a"][:, :, :], fl["a"][:, :, :], fl["b"][:, :, :], ALU.max))
                step(dve.tensor_tensor(fl["s"][:, :, :], fl["t1"][:, :, :], fl["a"][:, :, :], ALU.add))
                gs = RG["s"][:, :, :, 0]
                gmine = gs.unsqueeze(3).broadcast_to([P, TILES, NGRP, NGRP])
                gother = gs.unsqueeze(2).broadcast_to([P, TILES, NGRP, NGRP])
                own.done(dve.tensor_tensor(CG[:, 0], gother, gmine, ALU.is_gt))
                step(dve.tensor_tensor(CG[:, 1], gother, gmine, ALU.is_equal))
                tg = TIEG[:, :, :].unsqueeze(1).broadcast_to([P, TILES, NGRP, NGRP])
                step(dve.tensor_tensor(CG[:, 1], CG[:, 1], tg, ALU.mult))
                step(dve.tensor_tensor(CG[:, 0], CG[:, 0], CG[:, 1], ALU.add))
                step(dve.tensor_reduce(RKG[:, :, :], CG[:, 0], AX.X, ALU.add))
                step(dve.tensor_scalar(RKG[:, :, :], RKG[:, :, :], float(2), None, ALU.is_lt))
                rk = RKG[:, :, :].unsqueeze(3).broadcast_to([P, TILES, NGRP, GSZ])
                v4 = R["v"][:, :, :].rearrange("p t (g c) -> p t g c", g=NGRP)
                b44 = R["b"][:, :, :].rearrange("p t (g c) -> p t g c", g=NGRP)
                g4 = R["gm"][:, :, :].rearrange("p t (g c) -> p t g c", g=NGRP)
                own.done(dve.tensor_scalar(g4, rk, 1.0, -NEG, ALU.subtract, ALU.mult))
                step(dve.tensor_tensor(v4, b44, rk, ALU.mult))
                step(dve.tensor_tensor(R["v"][:, :, :], R["v"][:, :, :], R["gm"][:, :, :], ALU.add))

            mine_other = [P, TPB, EXPERTS, EXPERTS]
            halves = [slice(TPB * half, TPB * (half + 1)) for half in range(2)]
            better, equal = (w.rearrange("p (t e) c -> p t e c", e=EXPERTS) for w in CMP)

            def router_compare(half):
                h = halves[half]
                mine = R["v"][:, h, :].unsqueeze(3).broadcast_to(mine_other)
                other = R["v"][:, h, :].unsqueeze(2).broadcast_to(mine_other)
                own.done(dve.tensor_tensor(better[:, h], other, mine, ALU.is_gt))
                own.done(dve.tensor_tensor(equal[:, h], other, mine, ALU.is_equal))

            def router_weights(half):
                h = halves[half]
                after_own()
                step(dve.tensor_tensor(equal[:, h], equal[:, h], TIEB[:, :, :].unsqueeze(1).broadcast_to(mine_other), ALU.mult))
                step(dve.tensor_tensor(better[:, h], better[:, h], equal[:, h], ALU.add))
                step(dve.tensor_reduce(RK[:, h, :], better[:, h], AX.X, ALU.add))
                step(dve.tensor_scalar(RK[:, h, :], RK[:, h, :], float(TOPK), None, ALU.is_lt))
                step(dve.tensor_tensor(R["w"][:, h, :], RK[:, h, :], sc[:, h, :], ALU.mult))
                step(dve.tensor_reduce(WSUM[:, h], R["w"][:, h, :], AX.X, ALU.add))
                step(dve.tensor_scalar(WSUM[:, h], WSUM[:, h], 1e-20, None, ALU.add))
                step(dve.reciprocal(WREC[:, h], WSUM[:, h]))
                step(dve.tensor_tensor(R["c"][:, h, :], R["w"][:, h, :],
                                       WREC[:, h].unsqueeze(2).broadcast_to([P, TPB, EXPERTS]), ALU.mult))
                dve.tensor_scalar(R["c"][:, h, :], R["c"][:, h, :], 2.5, None, ALU.mult).then_inc(routed, 1)
                dve.wait_ge(routed, half + 1)

            def hidden(i, c, half, ffn=None):
                k = 8 * i + 2 * c + half
                dve.wait_ge(silu_done, k + 1)
                need(dve, h_lo, k - 1 if not isinstance(k, int) or k >= 2 else 0)
                if ffn is None:
                    ins = dve.tensor_tensor(HF[half], PS[:, BANK_U[half], :], SG[half], ALU.mult)
                else:
                    ins = dve.scalar_tensor_tensor(HF[half], PS[:, BANK_U[half], :], SSC[:, ffn, 1:2],
                                                   SG[half], ALU.mult, ALU.mult)
                ins.then_inc(h_done, 1)

            def add_down(i, c, half):
                k = 8 * i + 2 * c + half
                for t in range(TPB):
                    dve.wait_ge(y_ready, 4 * k + t + 1)
                    tile = half * TPB + t
                    y = PS[:, BANK_Y[t], 0:DM]
                    need(dve, y_added, 4 * k + t - 7 if not isinstance(k, int) or 4 * k + t >= 8 else 0)
                    if isinstance(i, int) and i == 0 and c == 0:
                        ins = dve.tensor_tensor(X[:, tile, :], y, X[:, tile, :], ALU.add)
                    else:
                        w = R["c"][:, tile, ds(4 * i + c - 1, 1)]
                        ins = dve.scalar_tensor_tensor(X[:, tile, :], y, w, X[:, tile, :],
                                                       ALU.mult, ALU.add)
                    ins.then_inc(y_added, 1)

            def add_output(tile):
                dve.wait_ge(out_scaled, tile + 1)
                dve.tensor_tensor(X[:, tile, :], X[:, tile, :], XN[:, tile, :], ALU.add).then_inc(out_ready, 1)

            def finish(half):
                k = 2 * (STREAM - 1) + half
                for t in range(TPB):
                    tile = half * TPB + t
                    dve.wait_ge(y_ready, 4 * k + t // 2 * 2 + 2)
                    y = PS[:, BANK_Y[tile // 2], tile % 2 * DM:(tile % 2 + 1) * DM]
                    dve.tensor_tensor(XN[:, tile, :], y, DSC[:, :], ALU.mult).then_inc(out_scaled, 1)
                add_output(half * TPB + 1)
                add_output(half * TPB + 3)

            for half in range(2):
                dve.wait_ge(x_in[half], 16)
                for t in range(TPB * half, TPB * (half + 1)):
                    statistics(t)
                variances(half)
            normalise(0, 0)
            split_weights(0)
            norm_lo(0, 0)
            attention(0)
            hidden(0, 0, 0)
            router_groups()
            hidden(0, 0, 1)
            router_compare(0)
            hidden(0, 1, 0)
            add_down(0, 0, 0)
            router_weights(0)
            hidden(0, 1, 1)
            add_down(0, 0, 1)
            router_compare(1)
            hidden(0, 2, 0)
            add_down(0, 1, 0)
            router_weights(1)
            hidden(0, 2, 1)
            add_down(0, 1, 1)
            with dve.Fori(0, 3) as i:
                for c in range(3, 7):
                    for half in range(2):
                        hidden(i, c, half)
                        add_down(i, c - 1, half)
            for c in range(15, 1 + EXPERTS):
                for half in range(2):
                    hidden(0, c, half)
                    add_down(0, c - 1, half)
            def last_statistics(half):
                dve.wait_ge(y_added, 8 * EXPERTS + 4 * half + 4)
                for t in range(TPB * half, TPB * (half + 1)):
                    statistics(t)
                variances(half)

            add_down(0, EXPERTS, 0)
            last_statistics(0)
            add_down(0, EXPERTS, 1)
            normalise(2, 0)
            norm_lo(2, 0)
            last_statistics(1)
            attention(1)
            for half in range(2):
                hidden(0, 17, half, 0)
            for c in range(18, STREAM):
                for half in range(2):
                    hidden(0, c, half, c - 17)
            for half in range(2):
                finish(half)

        @block.scalar
        def _(act):
            def root(l, half):
                tiles = slice(TPB * half, TPB * (half + 1))
                act.wait_ge(var_ready, 2 * l + half + 1)
                act.activation(SD[:, tiles], VE[:, tiles], ACT.Sqrt).then_inc(std_ready, 1)

            def take_hi(n, fill, bank):
                half, c = fill
                act.wait_ge(xT_ready, n + 1)
                act.copy(XT[0][:, c, half * SEQ:(half + 1) * SEQ], PS[:, bank, :]).then_inc(xT_hi_done, 1)

            def norm_hi(l, half):
                n = (0, 8, 12, 20)[l] + 2 * half
                for c in range(CH):
                    take_hi(n + c, (half, c), BANK_NORM[2 * half + c])

            def attention_step(layer, m, c):
                s0, s1 = c % 2, (c + 1) % 2
                has_c, has_b, has_a, has_o = (in_layer(c, d) for d in (0, 1, 2, -1))

                def take_kT(g, s, h):
                    p = h // 2
                    act.wait_ge(kT_ready, 2 * g + p + 1)
                    if h == 0:
                        need(act, s2_ready, 16 * g - 18)
                        need(act, zeroed, 1)
                    if h == 2:
                        need(act, s2_ready, 16 * g - 16)
                    rows = slice(64 * (h % 2), 64 * (h % 2) + 64)
                    act.copy(KT[s][rows, h, :], PS[rows, BANK_T[1 - p], :]).then_inc(kT_taken, 1)

                def take_mT(g, s, p):
                    act.wait_ge(mT_ready, 2 * g + p + 1)
                    act.copy(QT[s][:, p, :], PS[:, BANK_T[2], :]).then_inc(mT_taken, 1)

                def split_hi(part):
                    g = m + 2
                    src = QK[s0] if layer else ROPED[s0]
                    if part == 0:
                        act.wait_ge(qkv_taken if layer else rope_done, 4 * g + 4 if layer else 2 * g + 2)
                    need(act, mT_ready, 2 * g - 2)
                    need(act, kT_ready, 2 * g - 2)
                    if c == -2:
                        act.wait_ge(zeroed, 1)
                    n = TPB * HPG
                    if part == 0:
                        q2 = QS[s0][:, :, 0:2 * HD].rearrange("p r (a d) -> p r a d", a=2)
                        act.copy(q2, src[:, 0].unsqueeze(2).broadcast_to([P, n, 2, HD])).then_inc(stack_hi, 1)
                        return
                    k2 = KS[s0][:, :, :].rearrange("p r (a b d) -> p r a b d", a=2, b=2)[:, :, :, 0, :]
                    act.copy(k2, src[:, 1].unsqueeze(2).broadcast_to([P, n, 2, HD])).then_inc(stack_hi, 1)

                def exponentials(u):
                    kt = u // HPG
                    q0 = P * kt if layer else 0
                    act.wait_ge(s2_ready, 16 * m + u + 1)
                    act.activation(PT[:, u % NRING, q0:SEQ], PS[:, BANK_S2[u % 2], q0:SEQ], ACT.Exp,
                                   scale=SCALE).then_inc(exp_done, 1)

                for u in range(4 * TPB):
                    if has_c:
                        exponentials(u)
                    if has_c and u == 1:
                        take_mT(m, s0, 1)
                    if has_o and u == 3:
                        take_output(m - 1)
                    if has_b and u in (5, 6):
                        take_kT(m + 1, s1, u - 3)
                    if has_a and u in SPLIT_AT[layer]:
                        split_hi(SPLIT_AT[layer].index(u))
                    if has_b and u == 12:
                        take_mT(m + 1, s1, 0)
                    if layer == 0 and u == 10 and c in (GROUPS - 2, GROUPS - 1):
                        split_expert(0, c - GROUPS + 2)
                    if has_a and u - NEXT_TURNS_AT[layer] in (0, 1):
                        take_kT(m + 2, s0, u - NEXT_TURNS_AT[layer])
                if c == -2:
                    norm_hi(2 * layer, 1)

            def take_output(m):
                act.wait_ge(pv_done, 4 * m + 4)
                need(act, oT_ready, m)
                act.copy(OS[:, :], PS[:, BANK_O, :]).then_inc(o_taken, 1)

            def attention(layer):
                for c in range(-2, GROUPS):
                    attention_step(layer, GROUPS * layer + c, c)
                take_output(GROUPS * layer + GROUPS - 1)

            def split_weights(n):
                dst, src, s = ((WQKV, stage_qkv, wqkv_in), (WO, stage_wo, wo_in))[n % 2]
                act.wait_ge(s, 16 * (n // 2 + 1))
                act.copy(dst[0][:, :, :], src[:, :, :]).then_inc(wsplit_hi, 1)

            def split_expert(i, c):
                e = 4 * i + c
                act.wait_ge(stream_in[c % 2], 32 * i + 16 * (c // 2 + 1))
                need(act, y_ready, 8 * (e - 3) if not isinstance(e, int) or e >= 4 else 0)
                act.copy(WE[c % 4][0][:, :], stage_w[c % 2][:, :]).then_inc(we_hi, 1)

            def take_logits_t(half):
                act.wait_ge(lT_ready, half + 1)
                act.copy(LT[:, half, :], PS[0:EXPERTS, BANK_LT[half], :]).then_inc(lT_taken, 1)

            def silu(i, c, half, ffn=None):
                k = 8 * i + 2 * c + half
                act.wait_ge(gu_ready, k + 1)
                need(act, h_done, k - 1 if not isinstance(k, int) or k >= 2 else 0)
                act.activation(SG[half], PS[:, BANK_G[half], :], ACT.Silu,
                               scale=1.0 if ffn is None else SSC[:, ffn, 0:1]).then_inc(silu_done, 1)

            def hidden_hi(i, c, half):
                k = 8 * i + 2 * c + half
                act.wait_ge(h_done, k + 1)
                need(act, y_ready, 4 * (k - 3) if not isinstance(k, int) or k >= 4 else 0)
                act.copy(HR[(2 * c + half) % 4][0][:, :], HF[half]).then_inc(h_hi, 1)

            def unit(i, c, half, ffn=None):
                silu(i, c, half, ffn)
                hidden_hi(i, c, half)

            def expert(i, c):
                unit(i, c, 0)
                split_expert(i, c + 2)
                unit(i, c, 1)

            act.wait_ge(ident_loaded, 16)
            act.copy(ident_r[:, :], ident[:, :]).then_inc(ident_r_ready, 1)
            for half in range(2):
                root(0, half)
            split_weights(0)
            norm_hi(0, 0)
            split_weights(1)
            act.wait_ge(tables_in, 16 * 7)
            act.copy(GWT[0][:, :, :], GWS[:, :, :]).then_inc(consts_ready, 1)
            for layer in range(2):
                if layer:
                    root(2, 0)
                    norm_hi(2, 0)
                    root(2, 1)
                attention(layer)
                take_hi(12 * layer + 7, CTX_FILLS[3], BANK_CTX[3])
                if layer == 0:
                    split_expert(0, 2)
                for half in range(2):
                    root(2 * layer + 1, half)
                    norm_hi(2 * layer + 1, half)
                if layer == 0:
                    take_logits_t(0)
                    silu(0, 0, 0)
                    take_logits_t(1)
                    hidden_hi(0, 0, 0)
                    act.wait_ge(logits_ready, 1)
                    act.activation(R["e"][:, :, :].rearrange("p t e -> p (t e)"),
                                   PS[:, BANK_LOGITS, 0:TILES * EXPERTS], ACT.Exp,
                                   scale=-1.0).then_inc(router_exp, 1)
                    unit(0, 0, 1)
                    expert(0, 1)
                    with act.Fori(0, 3) as i:
                        for c in range(2, 6):
                            expert(i, c)
                    for c in range(14, 1 + EXPERTS):
                        expert(0, c)
                        if c >= EXPERTS - 1:
                            split_weights(c - EXPERTS + 3)
                else:
                    for c in range(17, STREAM):
                        for half in range(2):
                            unit(0, c, half, c - 17)
                            if half == 0 and c + 2 < STREAM:
                                split_expert(0, c + 2)

        @block.gpsimd
        def _(pool):
            own = Steps(pool_self)
            for s in range(2):
                own.done(pool.memset(QS[s][:, :, :].bitcast(F32), 0.0))
                own.done(pool.memset(KS[s][:, :, :].bitcast(F32), 0.0))
                own.done(pool.memset(KT[s][:, :, :].bitcast(F32), 0.0))
                own.done(pool.memset(VS[s][:, :, :, :], 0.0))
            pool.wait_ge(pool_self, own.n)
            for s in range(2):
                own.done(pool.memset(KS[s][:, :, 3 * HD:3 * HD + 2].bitcast(F32), 1.0))
                own.done(pool.memset(VS[s][:, :, :, HD:HD + 1], 1.0))
            pool.wait_ge(pool_self, own.n)
            pool.memset(RD[:, :], 0.0).then_inc(zeroed, 1)

            def split_weights(n):
                dst, src = ((WQKV, stage_qkv), (WO, stage_wo))[n % 2]
                pool.wait_ge(wsplit_hi, n + 1)
                pool.tensor_tensor(dst[1][:, :, :], src[:, :, :], dst[0][:, :, :].bitcast(F32),
                                   ALU.subtract).then_inc(wsplit_lo, 1)

            def split_expert(i, c):
                pool.wait_ge(we_hi, 4 * i + c + 1)
                pool.tensor_tensor(WE[c % 4][1][:, :], stage_w[c % 2][:, :],
                                   WE[c % 4][0][:, :].bitcast(F32), ALU.subtract).then_inc(we_lo, 1)

            def attention_step(layer, m, c):
                if in_layer(c, 1):
                    s1 = (c + 1) % 2
                    pool.wait_ge(qkv_taken, 4 * m + 8)
                    need(pool, pv_done, 4 * m)
                    pool.tensor_copy(VS[s1][:, :, :, 0:HD],
                                     QKV[s1][:, 2].rearrange("p (t h) d -> p t h d", h=HPG)).then_inc(v_stacked, 1)
                if layer and in_layer(c, 0):
                    mask_probs(m, 0)
                    mask_probs(m, 1)
                if in_layer(c, 2) and c > -2:
                    rope_and_split(layer, m, c)
                if layer and in_layer(c, 0):
                    mask_probs(m, 2)
                    mask_probs(m, 3)

            def mask_probs(m, kt):
                pool.wait_ge(exp_done, 16 * m + 4 * kt + 4)
                own = PT[:, 4 * kt % NRING:4 * kt % NRING + HPG, P * kt:P * (kt + 1)]
                pool.affine_select(out=own, in_=own, compare_op=ALU.is_ge, fill=0.0, base=0,
                                   pattern=[[0, HPG], [1, P]], channel_multiplier=-1).then_inc(probs_masked, 1)

            def rope_and_split(layer, m, c):
                g, s0 = m + 2, c % 2
                if layer == 0:
                    for unit in range(2):
                        rows = slice(2 * HPG * unit, 2 * HPG * (unit + 1))
                        pool.wait_ge(qkv_taken, 4 * g + 2 * unit + 2)
                        pool.wait_ge(rope_done, 2 * g + unit)
                        need(pool, stack_hi, 2 * g - 2)
                        pool.tensor_tensor(*rope_cos(s0, rows)).then_inc(rope_part, 1)
                        for j in range(2):
                            pool.tensor_tensor(*rope_sin(s0, rows, j)).then_inc(rope_part, 1)
                        pool.wait_ge(rope_part, 6 * g + 3 * unit + 3)
                        pool.tensor_tensor(*rope_sum(s0, rows)).then_inc(rope_done, 1)
                pool.wait_ge(stack_hi, 2 * g + 2)
                pool.memset(QS[s0][:, :, 3 * HD:3 * HD + 2].bitcast(F32), 0.0).then_inc(stack_lo, 1)
                pool.tensor_tensor(*q_lo(layer, s0)).then_inc(stack_lo, 1)
                pool.tensor_tensor(*k_lo(layer, s0)).then_inc(stack_lo, 1)

            def attention(layer):
                for c in range(-2, GROUPS):
                    attention_step(layer, GROUPS * layer + c, c)
                    if c == -2 and layer == 0:
                        pool.wait_ge(consts_ready, 1)
                        pool.tensor_tensor(GWT[1][:, :, :], GWS[:, :, :], GWT[0][:, :, :].bitcast(F32),
                                           ALU.subtract).then_inc(consts_ready, 1)
                    if c == GROUPS - 2:
                        add_bias(layer)
                    if c >= GROUPS - 2 and layer == 0:
                        split_expert(0, c - GROUPS + 2)

            def unit(i, c, half):
                k = 8 * i + 2 * c + half
                pool.wait_ge(h_hi, k + 1)
                H = HR[(2 * c + half) % 4]
                pool.tensor_tensor(H[1][:, :], HF[half], H[0][:, :].bitcast(F32),
                                   ALU.subtract).then_inc(h_lo, 1)

            def expert(i, c):
                unit(i, c, 0)
                split_expert(i, c + 2)
                unit(i, c, 1)

            def add_bias(layer):
                pool.wait_ge(rows_in, 32 * (layer + 1))
                pool.wait_ge(normed, 4 * layer + 2)
                pool.tensor_tensor(X[:, :, :], X[:, :, :],
                                   BO[:, :].unsqueeze(1).broadcast_to([P, TILES, DM]),
                                   ALU.add).then_inc(bias_added, 1)

            pool.wait_ge(rope_in, 16)
            attention(0)
            split_expert(0, 2)
            for half in range(2):
                unit(0, 0, half)
            expert(0, 1)
            with pool.Fori(0, 3) as i:
                for c in range(2, 6):
                    expert(i, c)
            for c in range(14, 1 + EXPERTS):
                expert(0, c)
                if c >= EXPERTS - 1:
                    split_weights(c - EXPERTS + 3)
            attention(1)
            for c in range(17, STREAM):
                for half in range(2):
                    unit(0, c, half)
                    if half == 0 and c + 2 < STREAM:
                        split_expert(0, c + 2)
            for tile in range(0, TILES, 2):
                pool.wait_ge(out_scaled, tile + 1)
                pool.tensor_tensor(X[:, tile, :], X[:, tile, :], XN[:, tile, :], ALU.add).then_inc(out_ready_even, 1)


def _chunks(w):
    return np.ascontiguousarray(w.reshape(-1, P, w.shape[1]).transpose(1, 0, 2))


def _by_group(w):
    lead = w.shape[:-1]
    w = w.reshape(*lead, 3, HEADS // HPG, HPG * HD)
    return np.ascontiguousarray(np.swapaxes(w, -3, -2)).reshape(*lead, 3 * DM)


def _stream(gate, up, down):
    g, u = (_chunks(w.T).reshape(P, CH * P) for w in (gate, up))
    return np.concatenate([g, u, down.T], axis=1)


def _rope_tables():
    inv = 1.0 / 10000.0 ** (np.arange(0, HD, 2, dtype=np.float32) / HD)
    freqs = np.outer(np.arange(SEQ, dtype=np.float32), inv)
    emb = np.concatenate([freqs, freqs], axis=-1)
    cos, sin = np.cos(emb).astype(np.float32), np.sin(emb).astype(np.float32)
    sin[:, :HD // 2] = -sin[:, :HD // 2]
    both = np.stack([cos, sin]).reshape(2, TPB, P, 1, HD)
    both = np.broadcast_to(both, (2, TPB, P, HPG, HD)).transpose(2, 0, 1, 3, 4)
    return np.ascontiguousarray(both).reshape(P, 2, TPB * HPG, HD)


def kernel(**inputs):
    import concourse.bacc as _bacc
    from concourse.bass_utils import run_bass_kernel_spmd as _run

    a = {k: np.asarray(v) for k, v in inputs.items()}
    tri = np.triu(np.ones((P, P), np.float32), 1) * np.float32(NEG)
    lower = [(np.arange(n)[None, :] < np.arange(n)[:, None]).astype(np.float32).ravel() for n in (EXPERTS, NGRP)]
    pad = FFN_CHUNKS * P - FFN_INTER
    gw, uw, dw = a["L1_ffn_gate_w"], a["L1_ffn_up_w"], a["L1_ffn_down_w"]
    gw, uw = (np.concatenate([w, np.zeros((pad, DM), np.float32)]) for w in (gw, uw))
    dw = np.concatenate([dw, np.zeros((DM, pad), np.float32)], axis=1)
    rows = [slice(c * P, (c + 1) * P) for c in range(FFN_CHUNKS)]
    stream = [_stream(a["L0_ffn_shared_gate"], a["L0_ffn_shared_up"], a["L0_ffn_shared_down"])]
    stream += [_stream(a["L0_ffn_gate_proj"][e], a["L0_ffn_up_proj"][e], a["L0_ffn_down_proj"][e]) for e in range(EXPERTS)]
    stream += [_stream(gw[r], uw[r], dw[:, r]) for r in rows]
    scales = [np.concatenate([a[n], np.zeros(pad, np.float32)]).reshape(FFN_CHUNKS, P).T for n in ("L1_ffn_gate_s", "L1_ffn_up_s")]
    w0 = np.concatenate([a["L0_attn_Wq"].T, a["L0_attn_Wk"].T, a["L0_attn_Wv"].T], axis=1)
    b0 = np.concatenate([a["L0_attn_bq"], a["L0_attn_bk"], a["L0_attn_bv"]])
    arrays = {
        "x": _chunks(a["L0_attn_x"].reshape(-1, DM)),
        "wqkv": np.stack([_chunks(_by_group(w0)), _chunks(_by_group(a["L1_attn_w_qkv"]))]),
        "bqkv": np.stack([_by_group(b0), _by_group(a["L1_attn_b_qkv"])]),
        "wo": np.stack([_chunks(a["L0_attn_Wo"].T), _chunks(a["L1_attn_w_proj"])]),
        "bo": np.stack([a["L0_attn_bo"], a["L1_attn_b_proj"]]),
        "rope": _rope_tables(),
        "mask": np.concatenate([np.zeros((P, SEQ - P), np.float32), tri], axis=1),
        "ident": np.eye(P, dtype=np.float32),
        "router_w": _chunks(a["L0_ffn_gate_weight"].T),
        "router_b": a["L0_ffn_expert_bias"],
        "ties": np.concatenate(lower)[None],
        "stream_w": np.stack(stream),
        "stream_scale": np.ascontiguousarray(np.stack(scales, axis=2)),
        "down_scale": a["L1_ffn_down_s"],
    }
    nc = _bacc.Bacc("TRN2", target_bir_lowering=False, num_devices=1)
    args = [nc.dram_tensor(f"in_{n}", v.shape, F32, kind="ExternalInput").ap() for n, v in arrays.items()]
    args.append(nc.dram_tensor("out_0", (P, TILES, DM), F32, kind="ExternalOutput").ap())
    two_layers(nc, *args)
    r = _run(nc, [{f"in_{n}": v for n, v in arrays.items()}], core_ids=[0])
    got = np.asarray(r.results[0]["out_0"])
    return np.ascontiguousarray(got.transpose(1, 0, 2)).reshape(BATCH, SEQ, DM)
```
